# Optimizing a Trainium2 kernel written in Bass

```python
import numpy as np
import jax
import jax.numpy as jnp

def _softmax(x, axis=-1):
    return jax.nn.softmax(x, axis=axis)

def _gelu(x):
    return jax.nn.gelu(x, approximate=True)

def _silu(x):
    return jax.nn.silu(x)

def _sigmoid(x):
    return jax.nn.sigmoid(x)

def _layernorm(x, axis=-1, eps=1e-05):
    m = jnp.mean(x, axis=axis, keepdims=True)
    v = jnp.var(x, axis=axis, keepdims=True)
    return (x - m) / jnp.sqrt(v + eps)

def _scatter_add(tgt, idx, src, axis=0):
    return tgt.at[idx].add(src)

def _segment_sum(src, seg, n):
    return jax.ops.segment_sum(src, seg, n)
kernel_name = 'mk_cond_resid_d2_seqx_r4_488e15'

def setup_inputs(seed: int=0):
    np.random.seed(seed)
    _w = jnp.asarray

    def _rec_inputs():
        import jax
        import jax.numpy as jnp
        _rk = jax.random.key(seed)
        x = -0.0003929 + 0.9999 * jax.random.normal(jax.random.fold_in(_rk, 1), (4, 512, 256), jnp.float32)
        _lenS = 512 - jax.random.randint(jax.random.fold_in(_rk, 7), (4,), 0, max(1, 512 // 4) + 1, jnp.int32)
        _lenS2 = 512 - jax.random.randint(jax.random.fold_in(_rk, 8), (4,), 0, max(1, 512 // 4) + 1, jnp.int32)
        cond_1024 = 0.00386106 + 1.00199 * jax.random.normal(jax.random.fold_in(_rk, 11), (4, 256), jnp.float32)
        return (x, cond_1024)
    x, cond_1024 = _rec_inputs()

    def _L0_cond_setup():
        import jax, jax.numpy as jnp
        import numpy as np
        RANK = 8
        LN_EPS = 1e-05
        key = jax.random.key(seed)
        ks = jax.random.split(key, 8)
        B, T, D = (16, 256, 256)
        A = 256
        I = 256
        OUT = D * RANK * 4
        s = 0.02
        return {'x': jax.random.normal(ks[0], (B, T, D), jnp.float32), 'ada_emb': jax.random.normal(ks[1], (B, A), jnp.float32), 'base_up': jax.random.normal(ks[2], (D, D), jnp.float32) * s, 'base_down': jax.random.normal(ks[3], (D, D), jnp.float32) * s, 'ln_gamma': jnp.ones((A,), jnp.float32), 'ln_beta': jnp.zeros((A,), jnp.float32), 'W1': jax.random.normal(ks[4], (A, I), jnp.float32) / np.sqrt(A), 'bias1': jnp.zeros((I,), jnp.float32), 'W2': jax.random.normal(ks[5], (I, OUT), jnp.float32) / np.sqrt(I), 'bias2': jnp.zeros((OUT,), jnp.float32)}
    _L0_cond_all = _L0_cond_setup()
    _L0_cond_in = {k: v for k, v in _L0_cond_all.items() if k in ('base_up', 'base_down', 'ln_gamma', 'ln_beta', 'W1', 'bias1', 'W2', 'bias2')}
    del _L0_cond_all

    def _L1_cond_setup():
        import jax, jax.numpy as jnp
        import numpy as np
        N, T, D, H = (64, 64, 256, 256)
        key = jax.random.key(seed)
        k1, k2, k3, k4 = jax.random.split(key, 4)
        x = jax.random.normal(k1, (N, T, D), dtype=jnp.float32)
        h0 = jax.random.normal(k2, (N, H), dtype=jnp.float32)
        Wx = jax.random.normal(k3, (D, H), dtype=jnp.float32) / jnp.sqrt(jnp.float32(D))
        Wh = jax.random.normal(k4, (H, H), dtype=jnp.float32) / jnp.sqrt(jnp.float32(H))
        b = jnp.zeros((H,), dtype=jnp.float32)
        return {'x': x, 'h0': h0, 'Wx': Wx, 'Wh': Wh, 'b': b}
    _L1_cond_all = _L1_cond_setup()
    _L1_cond_in = {k: v for k, v in _L1_cond_all.items() if k in ('Wx', 'Wh', 'b')}
    del _L1_cond_all
    return {'x': x, 'cond_1024': cond_1024, 'L0_cond_base_up': _L0_cond_in['base_up'], 'L0_cond_base_down': _L0_cond_in['base_down'], 'L0_cond_ln_gamma': _L0_cond_in['ln_gamma'], 'L0_cond_ln_beta': _L0_cond_in['ln_beta'], 'L0_cond_W1': _L0_cond_in['W1'], 'L0_cond_bias1': _L0_cond_in['bias1'], 'L0_cond_W2': _L0_cond_in['W2'], 'L0_cond_bias2': _L0_cond_in['bias2'], 'L1_cond_Wx': _L1_cond_in['Wx'], 'L1_cond_Wh': _L1_cond_in['Wh'], 'L1_cond_b': _L1_cond_in['b']}

def reference(x, cond_1024, L0_cond_base_up, L0_cond_base_down, L0_cond_ln_gamma, L0_cond_ln_beta, L0_cond_W1, L0_cond_bias1, L0_cond_W2, L0_cond_bias2, L1_cond_Wx, L1_cond_Wh, L1_cond_b):
    import jax
    import jax.numpy as jnp

    def _L0_cond_ref(x, ada_emb, base_up, base_down, ln_gamma, ln_beta, W1, bias1, W2, bias2):
        import jax, jax.numpy as jnp
        import numpy as np
        RANK = 8
        LN_EPS = 1e-05
        B, T, D = x.shape
        R = RANK
        mu = jnp.mean(ada_emb, axis=-1, keepdims=True)
        var = jnp.mean(jnp.square(ada_emb - mu), axis=-1, keepdims=True)
        c = (ada_emb - mu) / jnp.sqrt(var + LN_EPS) * ln_gamma + ln_beta
        h = jax.nn.gelu(c @ W1 + bias1, approximate=False)
        w = h @ W2 + bias2
        a1, b1, a2, b2 = [t.reshape(B, D, R) for t in jnp.split(w, 4, axis=-1)]
        u = jnp.einsum('btd,bdr->btr', x, a2)
        mid = jnp.einsum('btd,dl->btl', x, base_down) + jnp.einsum('btr,blr->btl', u, b2)
        mid = jax.nn.gelu(mid, approximate=False)
        v = jnp.einsum('blr,btl->btr', b1, mid)
        out = jnp.einsum('btl,kl->btk', mid, base_up) + jnp.einsum('bkr,btr->btk', a1, v)
        return x + out

    def _L1_cond_ref(x, h0, Wx, Wh, b):
        import jax, jax.numpy as jnp
        import numpy as np
        N, T, D, H = (64, 64, 256, 256)
        xW = jnp.einsum('ntd,dh->nth', x, Wx) + b

        def step(prev_h, xw_t):
            next_h = jnp.tanh(xw_t + prev_h @ Wh)
            return (next_h, next_h)
        _, hs = jax.lax.scan(step, h0, jnp.swapaxes(xW, 0, 1))
        return jnp.swapaxes(hs, 0, 1)
    x = x + _L0_cond_ref(x, cond_1024, L0_cond_base_up, L0_cond_base_down, L0_cond_ln_gamma, L0_cond_ln_beta, L0_cond_W1, L0_cond_bias1, L0_cond_W2, L0_cond_bias2)
    x = x + _L1_cond_ref(x, cond_1024, L1_cond_Wx, L1_cond_Wh, L1_cond_b)
    return x

_drawn_inputs = setup_inputs


def setup_inputs(seed=0):
    import zlib

    import numpy as np

    out = dict(_drawn_inputs(seed))
    spreads = {'L0_cond_ln_gamma': (1.0, 0.2),
     'L0_cond_ln_beta': (0.0, 0.1),
     'L0_cond_bias1': (0.0, 0.1),
     'L0_cond_bias2': (0.0, 0.1),
     'L1_cond_b': (0.0, 0.8)}
    factors = {'L0_cond_base_up': 4.833, 'L0_cond_base_down': 4.591, 'L1_cond_Wx': 8.0, 'L1_cond_Wh': 8.0}
    for name, (base, spread) in spreads.items():
        noise = np.random.default_rng([zlib.crc32(name.encode()), seed]).standard_normal(out[name].shape)
        drawn = base * np.exp(spread * noise) if base else spread * noise
        out[name] = jnp.asarray(drawn.astype(out[name].dtype))
    for name, factor in factors.items():
        out[name] = (out[name] * factor).astype(out[name].dtype)
    return out
```

```python
from contextlib import ExitStack

import concourse.bass as bass
from concourse import mybir

F32 = mybir.dt.float32
BF16 = mybir.dt.bfloat16
ALU = mybir.AluOpType
ACT = mybir.ActivationFunctionType
AX = mybir.AxisListType

P = 128
RANK = 8
LN_EPS = 1e-5
TS = 16
PAIR = 2 * TS


def adaptive_lowrank_then_recurrence(nc, x, cond, base_up, base_down, ln_gamma, ln_beta, W1, bias1, W2,
                                     bias2, Wx, Wh, b_rnn, out):
    B, T, D = x.shape
    K2 = D // P
    NTYPE = 4
    A1, B1, A2, B2 = range(NTYPE)
    Q = B * RANK
    WCOL = D * RANK
    CH = 512
    NCH = WCOL // CH
    NTT = T // P
    NTILE = T // TS
    NPAIR = NTILE // 2
    TC = TS * B
    assert B * PAIR == P
    assert Q == 32 and K2 == 2 and D == 256 and T == 512 and NCH == 4

    with ExitStack() as ctx:
        def sb(name, shape, dt=F32):
            return ctx.enter_context(nc.sbuf_tensor(name, shape, dt))

        def sem(name):
            return ctx.enter_context(nc.semaphore(name))

        bank = [ctx.enter_context(nc.psum_tensor(f"bank{i}", [P, 512], F32)) for i in range(8)]

        cond_sb = sb("cond_sb", [B, D])
        gamma_sb = sb("gamma_sb", [B, D])
        beta_sb = sb("beta_sb", [B, D])
        w1_sb = sb("w1_sb", [P, K2, D])
        bias1_sb = sb("bias1_sb", [P, K2])
        bias2_sb = sb("bias2_sb", [P, WCOL])
        w2_sb = sb("w2_sb", [P, K2, NTYPE, WCOL])
        x_sb = sb("x_sb", [P, B, NTT, D])
        up_sb = sb("up_sb", [P, K2, D])
        down_sb = sb("down_sb", [P, K2, D])
        wx_sb = sb("wx_sb", [P, K2, D])
        wh_sb = sb("wh_sb", [P, K2, D])
        brow = sb("brow", [1, D])

        zeros = sb("zeros", [P, P])
        ident = sb("ident", [P, P])
        sel3 = sb("sel3", [P, P // RANK, RANK])
        rmask = sb("rmask", [P, RANK])
        bmask = sb("bmask", [P, B])
        ones_row = sb("ones_row", [1, TC])

        stats = sb("stats", [B, 6])
        mv = sb("mv", [B, 2])
        std = sb("std", [B, 1])
        rstd = sb("rstd", [B, 1])
        cn = sb("cn", [B, D])
        eps_sb = sb("eps_sb", [B, 1])
        cT = sb("cT", [P, K2, B])
        gT = sb("gT", [P, K2, B])
        gRep = sb("gRep", [P, K2, B, RANK])
        bmul = sb("bmul", [P, WCOL])
        bias_f = sb("bias_f", [P, D])
        wmul = sb("wmul", [P, 2, CH])
        fac = sb("fac", [P, D])
        facm = sb("facm", [P, B, D])
        b1m = sb("b1m", [Q, B, D])
        b2s = sb("b2s", [P, D])
        upT = sb("upT", [P, K2, D])
        wd = sb("wd", [P, B, K2, D])
        wu = sb("wu", [P, B, K2, D])

        xT = sb("xT", [P, K2, B, T])
        midT = sb("midT", [P, 2, K2, T])
        x2T = sb("x2T", [P, K2, T * B])

        whp = [sb(f"whp{i}", [P, K2, D], BF16) for i in range(3)]
        wres = sb("wres", [P, 2, K2, D])
        h_ring = sb("h_ring", [P, K2, PAIR, B])
        r_ring = sb("r_ring", [P, K2, 2, B])
        l_ring = sb("l_ring", [P, K2, 2, B], BF16)
        y_sb = sb("y_sb", [P, K2, B, PAIR])
        o_sb = sb("o_sb", [P, D])
        h_hi = h_ring[:].bitcast(BF16).rearrange("p k s (b w) -> p k s b w", w=2)[:, :, :, :, 1]
        r_hi = r_ring[:].bitcast(BF16).rearrange("p k s (b w) -> p k s b w", w=2)[:, :, :, :, 1]

        ld_cond = sem("ld_cond")
        ld_bias2 = sem("ld_bias2")
        ld_x = [sem(f"ld_x{b}") for b in range(B)]
        ld_base = sem("ld_base")
        ld_w2 = [sem(f"ld_w2_{c}") for c in range(NCH)]
        ld_rnn = sem("ld_rnn")
        const_ready = sem("const_ready")
        pool_step = sem("pool_step")
        dve_step = sem("dve_step")
        var_ready = sem("var_ready")
        std_ready = sem("std_ready")
        cn_ready = sem("cn_ready")
        condT_ready = sem("condT_ready")
        cT_psum = sem("cT_psum")
        cT_ready = sem("cT_ready")
        hpre_ready = sem("hpre_ready")
        g_ready = sem("g_ready")
        grep_ready = sem("grep_ready")
        tr_ready = sem("tr_ready")
        tr_dve = sem("tr_dve")
        tr_act = sem("tr_act")
        w_ready = sem("w_ready")
        facm_ready = sem("facm_ready")
        b1_ready = sem("b1_ready")
        b2_ready = sem("b2_ready")
        wd_psum = sem("wd_psum")
        wd_ready = sem("wd_ready")
        wu_psum = sem("wu_psum")
        wu_ready = sem("wu_ready")
        mid_psum = sem("mid_psum")
        mid_ready = sem("mid_ready")
        up_psum = sem("up_psum")
        x2_ready = sem("x2_ready")
        whp_ready = sem("whp_ready")
        h_ready = sem("h_ready")
        r_ready = sem("r_ready")
        l_ready = sem("l_ready")
        z_ready = sem("z_ready")
        y_ready = sem("y_ready")
        yT_ready = sem("yT_ready")
        o_ready = sem("o_ready")
        out_done = sem("out_done")

        block = ctx.enter_context(nc.Block())

        NTR = B * K2 + 1

        def tr_bank(g):
            return bank[4 + g % 3]

        def slot_before(s):
            return (s - 1) % PAIR

        def over_pairs(eng, body):
            body(0, True, False)
            body(1, False, False)
            with eng.Fori(2, NPAIR - 1) as pair:
                body(pair, False, False)
            body(NPAIR - 1, False, True)

        @block.sync
        def _(sp):
            sp.dma_start(cond_sb[:], cond).then_inc(ld_cond, 16)
            sp.dma_start(gamma_sb[:], ln_gamma.partition_broadcast(B)).then_inc(ld_cond, 16)
            sp.dma_start(beta_sb[:], ln_beta.partition_broadcast(B)).then_inc(ld_cond, 16)
            sp.dma_start(w1_sb[:], W1.rearrange("(k p) n -> p k n", p=P)).then_inc(ld_cond, 16)
            sp.dma_start(bias1_sb[:], bias1.rearrange("(k p) -> p k", p=P),
                         allow_slow_non_contiguous=True).then_inc(ld_cond, 16)
            for j in range(NTYPE):
                sp.dma_start(bias2_sb[Q * j:Q * (j + 1), :],
                             bias2[WCOL * j:WCOL * (j + 1)].partition_broadcast(Q)).then_inc(ld_bias2, 16)
            for b in range(B):
                sp.dma_start(x_sb[:, b], x[b].rearrange("(n p) d -> p n d", p=P)).then_inc(ld_x[b], 16)
            sp.dma_start(up_sb[:], base_up.rearrange("(k p) n -> p k n", p=P)).then_inc(ld_base, 16)
            sp.dma_start(down_sb[:], base_down.rearrange("(k p) n -> p k n", p=P)).then_inc(ld_base, 16)
            w2v = W2.rearrange("(k p) (j n) -> k p j n", p=P, j=NTYPE)
            for c in range(NCH):
                for k in range(K2):
                    sp.dma_start(w2_sb[:, k, :, CH * c:CH * (c + 1)],
                                 w2v[k, :, :, CH * c:CH * (c + 1)]).then_inc(ld_w2[c], 16)
            sp.dma_start(wh_sb[:], Wh.rearrange("(k p) n -> p k n", p=P)).then_inc(ld_rnn, 16)
            sp.dma_start(wx_sb[:], Wx.rearrange("(k p) n -> p k n", p=P)).then_inc(ld_rnn, 16)
            sp.dma_start(brow[:], b_rnn.partition_broadcast(1)).then_inc(ld_rnn, 16)

            def write_pair(done_pair):
                sp.wait_ge(o_ready, done_pair + 1)
                for b in range(B):
                    sp.dma_start(out[b, bass.ds(done_pair * PAIR, PAIR), :],
                                 o_sb[PAIR * b:PAIR * (b + 1), :]).then_inc(out_done, 16)

            def output(pair, first, last):
                if not first:
                    write_pair(pair - 1)
                if last:
                    write_pair(pair)

            over_pairs(sp, output)
            sp.wait_ge(out_done, 16 * B * NPAIR)

        @block.gpsimd
        def _(pool):
            nc.gpsimd.memset(zeros[:], 0.0).then_inc(pool_step, 1)
            nc.gpsimd.memset(ones_row[:], 1.0).then_inc(const_ready, 1)
            nc.gpsimd.memset(eps_sb[:], LN_EPS).then_inc(const_ready, 1)
            pool.wait_ge(pool_step, 1)
            nc.gpsimd.affine_select(out=ident[:], in_=zeros[:], compare_op=ALU.not_equal, fill=1.0, base=0,
                                    pattern=[[-1, P]], channel_multiplier=1).then_inc(const_ready, 1)
            nc.gpsimd.affine_select(out=sel3[:].rearrange("p q r -> p (q r)"), in_=zeros[:],
                                    compare_op=ALU.not_equal, fill=1.0, base=0,
                                    pattern=[[-RANK, P // RANK], [-1, RANK]],
                                    channel_multiplier=1).then_inc(const_ready, 1)
            pool.wait_ge(ld_rnn, 48)
            nc.gpsimd.tensor_copy(whp[0][:], wh_sb[:]).then_inc(pool_step, 1)
            pool.wait_ge(pool_step, 2)
            nc.gpsimd.tensor_tensor(wres[:, 0], wh_sb[:], whp[0][:], ALU.subtract).then_inc(pool_step, 1)
            pool.wait_ge(pool_step, 3)
            nc.gpsimd.tensor_copy(whp[1][:], wres[:, 0]).then_inc(pool_step, 1)
            pool.wait_ge(pool_step, 4)
            nc.gpsimd.tensor_tensor(wres[:, 1], wres[:, 0], whp[1][:], ALU.subtract).then_inc(pool_step, 1)
            pool.wait_ge(pool_step, 5)
            nc.gpsimd.tensor_copy(whp[2][:], wres[:, 1]).then_inc(whp_ready, 1)

        @block.scalar
        def _(act):
            act.wait_ge(var_ready, 1)
            act.wait_ge(const_ready, 4)
            nc.scalar.activation(std[:], mv[:, 1:2], ACT.Sqrt, bias=eps_sb[:]).then_inc(std_ready, 1)
            act.wait_ge(condT_ready, 1)
            for m in range(K2):
                nc.scalar.copy(h_ring[:, m, PAIR - 1, :], bank[7][:, B * m:B * (m + 1)]).then_inc(h_ready, 1)

            def move_transposes(g):
                act.wait_ge(tr_ready, g + 1)
                nc.scalar.copy(xT[:, g % K2, g // K2, :], tr_bank(g)[:]).then_inc(tr_act, 1)

            move_transposes(1)
            act.wait_ge(hpre_ready, 1)
            for m in range(K2):
                nc.scalar.activation(gT[:, m, :], bank[7][:, 32 + B * m:32 + B * (m + 1)], ACT.Gelu,
                                     bias=bias1_sb[:, m:m + 1]).then_inc(g_ready, 1)
            for g in range(3, B * K2, 2):
                move_transposes(g)
            act.wait_ge(facm_ready, 1)
            nc.scalar.copy(b1m[:], facm[Q * B1:Q * (B1 + 1)]).then_inc(b1_ready, 1)
            for b in range(B):
                for m in range(K2):
                    act.wait_ge(mid_psum, K2 * b + m + 1)
                    if b >= 2 and m == 0:
                        act.wait_ge(up_psum, K2 * (b - 1))
                    nc.scalar.activation(midT[:, b % 2, m, :], bank[4 + 2 * (b % 2) + m][:],
                                         ACT.Gelu).then_inc(mid_ready, 1)

            def move_rows(done_pair):
                act.wait_ge(yT_ready, done_pair + 1)
                if not (isinstance(done_pair, int) and done_pair == 0):
                    act.wait_ge(out_done, 16 * B * done_pair)
                nc.scalar.copy(o_sb[:], bank[4][:, 0:D]).then_inc(o_ready, 1)

            def states(pair, first, last):
                for s in range(PAIR):
                    if s % TS == 0 and not first:
                        act.wait_ge(y_ready, 2 * pair + s // TS - 1)
                    for m in range(K2):
                        act.wait_ge(z_ready, 2 * PAIR * pair + 2 * s + m + 1)
                        zt = bank[2 * (s // TS) + m][:, B * (s % TS):B * (s % TS + 1)]
                        nc.scalar.activation(h_ring[:, m, s, :], zt, ACT.Tanh).then_inc(h_ready, 1)
                    if s == 6 and not first:
                        move_rows(pair - 1)
                if last:
                    move_rows(pair)

            over_pairs(act, states)

        @block.vector
        def _(dve):
            steps = [0]

            def then_wait(ins):
                steps[0] += 1
                ins.then_inc(dve_step, 1)
                dve.wait_ge(dve_step, steps[0])

            dve.wait_ge(ld_cond, 80)
            then_wait(nc.vector.bn_stats(stats[:], cond_sb[:]))
            nc.vector.bn_aggr(mv[:], stats[:]).then_inc(var_ready, 1)
            dve.wait_ge(std_ready, 1)
            then_wait(nc.vector.reciprocal(rstd[:], std[:]))
            then_wait(nc.vector.tensor_scalar(cn[:], cond_sb[:], mv[:, 0:1], rstd[:], ALU.subtract, ALU.mult))
            then_wait(nc.vector.tensor_tensor(cn[:], cn[:], gamma_sb[:], ALU.mult))
            nc.vector.tensor_tensor(cn[:], cn[:], beta_sb[:], ALU.add).then_inc(cn_ready, 1)
            dve.wait_ge(const_ready, 4)
            nc.vector.tensor_reduce(rmask[:], sel3[:].rearrange("p q r -> p r q"), AX.X, ALU.add)
            then_wait(nc.vector.tensor_reduce(bmask[:], sel3[:].rearrange("p (j b) r -> p b j r", b=B), AX.XY,
                                              ALU.add))
            dve.wait_ge(cT_psum, 1)
            nc.vector.tensor_copy(cT[:].rearrange("p k b -> p (k b)"),
                                  bank[7][:, 16:16 + K2 * B]).then_inc(cT_ready, 1)

            def move_transposes(g):
                dve.wait_ge(tr_ready, g + 1)
                dst = xT[:, g % K2, g // K2, :] if g < B * K2 else upT[:].rearrange("p k n -> p (k n)")
                nc.vector.tensor_copy(dst, tr_bank(g)[:]).then_inc(tr_dve, 1)

            move_transposes(0)
            dve.wait_ge(g_ready, 2)
            nc.vector.tensor_copy(gRep[:], gT[:].unsqueeze(3).broadcast_to([P, K2, B, RANK])).then_inc(grep_ready, 1)
            for g in range(2, NTR, 2):
                move_transposes(g)

            def keep_rank(dst, src, tmp, n, srcsem=None):
                mask = rmask[:].unsqueeze(1).broadcast_to([P, n, RANK])
                then_wait(nc.vector.tensor_tensor(tmp.rearrange("p (d r) -> p d r", r=RANK),
                                                  src.rearrange("p (d r) -> p d r", r=RANK), mask, ALU.mult))
                then_wait(nc.vector.tensor_reduce(dst, tmp.rearrange("p (d r) -> p d r", r=RANK), AX.X, ALU.add))

            dve.wait_ge(ld_bias2, 64)
            keep_rank(bias_f[:], bias2_sb[:], bmul[:], D)
            DC = CH // RANK
            for c in range(NCH):
                dve.wait_ge(w_ready, c + 1)
                keep_rank(fac[:, DC * c:DC * (c + 1)], bank[c][:], wmul[:, c % 2], DC)
            then_wait(nc.vector.tensor_tensor(fac[:], fac[:], bias_f[:], ALU.add))
            nc.vector.tensor_copy(b2s[Q * A2:Q * (A2 + 1)], fac[Q * B2:Q * (B2 + 1)]).then_inc(b2_ready, 1)
            nc.vector.tensor_tensor(facm[:], fac[:].unsqueeze(1).broadcast_to([P, B, D]),
                                    bmask[:].unsqueeze(2).broadcast_to([P, B, D]), ALU.mult).then_inc(facm_ready, 1)
            dve.wait_ge(ld_base, 32)
            for b in range(B):
                dve.wait_ge(wd_psum, b + 1)
                nc.vector.tensor_tensor(wd[:, b].rearrange("p k n -> p (k n)"), bank[4 + b][:],
                                        down_sb[:].rearrange("p k n -> p (k n)"), ALU.add).then_inc(wd_ready, 1)
            for b in range(B):
                dve.wait_ge(wu_psum, b + 1)
                nc.vector.tensor_tensor(wu[:, b].rearrange("p k n -> p (k n)"), bank[b][:],
                                        upT[:].rearrange("p k n -> p (k n)"), ALU.add).then_inc(wu_ready, 1)
            for b in range(B):
                for n in range(K2):
                    dve.wait_ge(up_psum, K2 * b + n + 1)
                    nc.vector.scalar_tensor_tensor(
                        out=x2T[:, n].rearrange("p (t b) -> p b t", b=B)[:, b], in0=xT[:, n, b, :], scalar=2.0,
                        in1=bank[2 * (b % 2) + n][:], op0=ALU.mult, op1=ALU.add).then_inc(x2_ready, 1)

            def output_sum(p, col0, in_pair):
                if p == 0 and not (isinstance(in_pair, int) and in_pair == 0):
                    dve.wait_ge(yT_ready, in_pair)
                for k in range(K2):
                    last = nc.vector.tensor_tensor(
                        y_sb[:, k, :, TS * p:TS * (p + 1)],
                        x2T[:, k, bass.ds(col0, TC)].rearrange("p (t b) -> p b t", b=B),
                        h_ring[:, k, TS * p:TS * (p + 1), :].rearrange("p t b -> p b t"), ALU.add)
                last.then_inc(y_ready, 1)

            def residues(pair, first, last):
                for s in range(PAIR):
                    q = s % 2
                    before = slot_before(s)
                    for k in range(K2):
                        dve.wait_ge(h_ready, 2 * PAIR * pair + 2 * s + k + 1)
                        nc.vector.tensor_tensor(r_ring[:, k, q, :], h_ring[:, k, before, :], h_hi[:, k, before, :],
                                                ALU.subtract).then_inc(r_ready, 1)
                    for k in range(K2):
                        dve.wait_ge(r_ready, 2 * PAIR * pair + 2 * s + k + 1)
                        nc.vector.tensor_tensor(l_ring[:, k, q, :], r_ring[:, k, q, :], r_hi[:, k, q, :],
                                                ALU.subtract).then_inc(l_ready, 1)
                    if s == 2 and not first:
                        output_sum(1, (PAIR * pair - TS) * B, pair - 1)
                    if s == TS + 2:
                        output_sum(0, PAIR * pair * B, pair)
                if last:
                    dve.wait_ge(h_ready, 2 * PAIR * (pair + 1) + 2)
                    output_sum(1, (PAIR * pair + TS) * B, pair)

            over_pairs(dve, residues)

        @block.tensor
        def _(pe):
            pe.wait_ge(const_ready, 4)
            pe.wait_ge(ld_cond, 80)
            for k in range(K2):
                last = nc.tensor.transpose(bank[7][:, B * k:B * (k + 1)], cond_sb[:, P * k:P * (k + 1)],
                                           ident[0:B, 0:B])
            last.then_inc(condT_ready, 1)

            def transposes(g):
                if g >= 3:
                    prev = g - 3
                    pe.wait_ge(tr_dve if prev % 2 == 0 else tr_act, prev // 2 + 1)
                for i in range(4):
                    if g < B * K2:
                        src = x_sb[:, g // K2, i, P * (g % K2):P * (g % K2 + 1)]
                    else:
                        src = up_sb[:, i % 2, P * (i // 2):P * (i // 2 + 1)]
                    last = nc.tensor.transpose(tr_bank(g)[:, P * i:P * (i + 1)], src, ident[:])
                last.then_inc(tr_ready, 1)

            pe.wait_ge(cn_ready, 1)
            pe.wait_ge(h_ready, 2)
            for k in range(K2):
                last = nc.tensor.transpose(bank[7][:, 16 + B * k:16 + B * (k + 1)], cn[:, P * k:P * (k + 1)],
                                           ident[0:B, 0:B])
            last.then_inc(cT_psum, 1)
            pe.wait_ge(ld_x[0], 16)
            transposes(0)
            transposes(1)
            pe.wait_ge(cT_ready, 1)
            for m in range(K2):
                for k in range(K2):
                    last = nc.tensor.matmul(bank[7][:, 32 + B * m:32 + B * (m + 1)], w1_sb[:, k, P * m:P * (m + 1)],
                                            cT[:, k, :], start=(k == 0), stop=(k == K2 - 1))
            last.then_inc(hpre_ready, 1)
            for g in range(2, NTR):
                if g < B * K2 and g % K2 == 0:
                    pe.wait_ge(ld_x[g // K2], 16)
                if g == B * K2:
                    pe.wait_ge(ld_base, 32)
                transposes(g)
            pe.wait_ge(grep_ready, 1)
            for c in range(NCH):
                pe.wait_ge(ld_w2[c], 32)
                for k in range(K2):
                    for j in range(NTYPE):
                        last = nc.tensor.matmul(bank[c][Q * j:Q * (j + 1), :],
                                                gRep[:, k].rearrange("p b r -> p (b r)"),
                                                w2_sb[:, k, j, CH * c:CH * (c + 1)], start=(k == 0),
                                                stop=(k == K2 - 1))
                last.then_inc(w_ready, 1)
            pe.wait_ge(b2_ready, 1)
            pe.wait_ge(facm_ready, 1)
            pe.wait_ge(tr_dve, NTR // 2 + 1)
            pe.wait_ge(tr_act, B * K2 // 2)
            for b in range(B):
                for k in range(K2):
                    last = nc.tensor.matmul(bank[4 + b][:, D * k:D * (k + 1)],
                                            facm[Q * A2:Q * (A2 + 1), b, P * k:P * (k + 1)],
                                            b2s[Q * A2:Q * (A2 + 1), :], start=True, stop=True)
                last.then_inc(wd_psum, 1)
            pe.wait_ge(b1_ready, 1)
            for b in range(B):
                for k in range(K2):
                    last = nc.tensor.matmul(bank[b][:, D * k:D * (k + 1)], b1m[:, b, P * k:P * (k + 1)],
                                            fac[Q * A1:Q * (A1 + 1), :], start=True, stop=True)
                last.then_inc(wu_psum, 1)

            def down(b):
                pe.wait_ge(wd_ready, min(b + 3, B) if b < 2 else B)
                if b >= 2:
                    pe.wait_ge(mid_ready, K2 * (b - 1))
                elif b == 0:
                    pe.wait_ge(wd_ready, 2)
                for m in range(K2):
                    for k in range(K2):
                        last = nc.tensor.matmul(bank[4 + 2 * (b % 2) + m][:], wd[:, b, k, P * m:P * (m + 1)],
                                                xT[:, k, b, :], start=(k == 0), stop=(k == K2 - 1))
                    last.then_inc(mid_psum, 1)

            def up(b):
                pe.wait_ge(mid_ready, K2 * (b + 1))
                pe.wait_ge(wu_ready, B)
                if b >= 2:
                    pe.wait_ge(x2_ready, K2 * (b - 1))
                for n in range(K2):
                    for k in range(K2):
                        last = nc.tensor.matmul(bank[2 * (b % 2) + n][:], wu[:, b, k, P * n:P * (n + 1)],
                                                midT[:, b % 2, k, :], start=(k == 0), stop=(k == K2 - 1))
                    last.then_inc(up_psum, 1)

            down(0)
            for b in range(1, B):
                down(b)
                up(b - 1)
            up(B - 1)

            def input_part(p, col0, i):
                m, k = i // 3, i % 3 - 1
                zb = bank[2 * p + m][:, 0:TC]
                if k < 0:
                    nc.tensor.matmul(zb, brow[0:1, P * m:P * (m + 1)], ones_row[:], start=True, stop=False,
                                     skip_group_check=True)
                else:
                    nc.tensor.matmul(zb, wx_sb[:, k, P * m:P * (m + 1)], x2T[:, k, bass.ds(col0, TC)],
                                     start=False, stop=False, skip_group_check=True)

            def output_transposes(done_pair):
                pe.wait_ge(y_ready, 2 * done_pair + 2)
                if not (isinstance(done_pair, int) and done_pair == 0):
                    pe.wait_ge(o_ready, done_pair)
                for n in range(K2):
                    last = nc.tensor.transpose(bank[4][:, P * n:P * (n + 1)],
                                               y_sb[:, n].rearrange("p b t -> p (b t)"), ident[:])
                last.then_inc(yT_ready, 1)

            def recurrence(pair, first, last):
                for s in range(PAIR):
                    p, q, before = s // TS, s % 2, slot_before(s)
                    cols = slice(B * (s % TS), B * (s % TS + 1))
                    done = 2 * PAIR * pair + 2 * s

                    def product(part, k, m, rhs, stop=False):
                        return nc.tensor.matmul(bank[2 * p + m][:, cols], whp[part][:, k, P * m:P * (m + 1)], rhs,
                                                start=False, stop=stop, skip_group_check=True)

                    pe.wait_ge(h_ready, done + 1)
                    for part in range(3):
                        product(part, 0, 0, h_hi[:, 0, before, :])
                    pe.wait_ge(h_ready, done + 2)
                    for k, m in ((0, 1), (1, 0), (1, 1)):
                        for part in range(3):
                            product(part, k, m, h_hi[:, k, before, :])
                    pe.wait_ge(r_ready, done + 1)
                    for m in range(K2):
                        for part in range(2):
                            product(part, 0, m, r_hi[:, 0, q, :])
                    pe.wait_ge(r_ready, done + 2)
                    for part in range(2):
                        product(part, 1, 0, r_hi[:, 1, q, :])
                    pe.wait_ge(l_ready, done + 1)
                    product(0, 0, 0, l_ring[:, 0, q, :])
                    pe.wait_ge(l_ready, done + 2)
                    product(0, 1, 0, l_ring[:, 1, q, :], stop=True).then_inc(z_ready, 1)
                    for part in range(2):
                        product(part, 1, 1, r_hi[:, 1, q, :])
                    product(0, 0, 1, l_ring[:, 0, q, :])
                    product(0, 1, 1, l_ring[:, 1, q, :], stop=True).then_inc(z_ready, 1)

                    st = s % TS
                    if 8 <= st < 14 and not (last and p == 1):
                        input_part(1 - p, (PAIR * pair + TS * (p + 1)) * B, st - 8)
                    if s == 4 and not first:
                        output_transposes(pair - 1)
                if last:
                    output_transposes(pair)

            pe.wait_ge(ld_rnn, 48)
            pe.wait_ge(x2_ready, K2 * B)
            for i in range(6):
                input_part(0, 0, i)
            pe.wait_ge(whp_ready, 1)
            over_pairs(pe, recurrence)


_INS = ["x", "cond_1024", "L0_cond_base_up", "L0_cond_base_down", "L0_cond_ln_gamma", "L0_cond_ln_beta",
        "L0_cond_W1", "L0_cond_bias1", "L0_cond_W2", "L0_cond_bias2", "L1_cond_Wx", "L1_cond_Wh", "L1_cond_b"]


def kernel(**inputs):
    import numpy as _np
    import concourse.bacc as _bacc
    from concourse import mybir as _mybir
    from concourse.bass_utils import run_bass_kernel_spmd as _run

    nc = _bacc.Bacc("TRN2", target_bir_lowering=False, num_devices=1)
    arrays, args = {}, []
    for name in _INS:
        a = _np.ascontiguousarray(inputs[name])
        arrays[f"in_{name}"] = a
        args.append(nc.dram_tensor(f"in_{name}", a.shape, _mybir.dt.from_np(a.dtype), kind="ExternalInput").ap())
    shape = inputs["x"].shape
    args.append(nc.dram_tensor("out_0", shape, _mybir.dt.float32, kind="ExternalOutput").ap())
    adaptive_lowrank_then_recurrence(nc, *args)
    r = _run(nc, [arrays], core_ids=[0])
    return r.results[0]["out_0"]
```

```python
from contextlib import ExitStack

import concourse.bass as bass
from concourse import mybir

F32 = mybir.dt.float32
BF16 = mybir.dt.bfloat16
ALU = mybir.AluOpType
ACT = mybir.ActivationFunctionType
AX = mybir.AxisListType

P = 128
RANK = 8
LN_EPS = 1e-5
TS = 16
PAIR = 2 * TS
NPART = 3


def adaptive_lowrank_then_recurrence(nc, x, cond, base_up, base_down, ln_gamma, ln_beta, W1, bias1, W2,
                                     bias2, Wx, Wh, b_rnn, out):
    B, T, D = x.shape
    K2 = D // P
    NTYPE = 4
    A1, B1, A2, B2 = range(NTYPE)
    Q = B * RANK
    WCOL = D * RANK
    CH = 512
    NCH = WCOL // CH
    NTT = T // P
    NTILE = T // TS
    NPAIR = NTILE // 2
    TC = TS * B
    assert B * PAIR == P
    assert Q == 32 and K2 == 2 and D == 256 and T == 512 and NCH == 4

    with ExitStack() as ctx:
        def sb(name, shape, dt=F32):
            return ctx.enter_context(nc.sbuf_tensor(name, shape, dt))

        def sem(name):
            return ctx.enter_context(nc.semaphore(name))

        bank = [ctx.enter_context(nc.psum_tensor(f"bank{i}", [P, 512], F32)) for i in range(8)]

        cond_sb = sb("cond_sb", [B, D])
        gamma_sb = sb("gamma_sb", [B, D])
        beta_sb = sb("beta_sb", [B, D])
        w1_sb = sb("w1_sb", [P, K2, D])
        bias1_sb = sb("bias1_sb", [P, K2])
        bias2_sb = sb("bias2_sb", [P, WCOL])
        w2_sb = sb("w2_sb", [P, K2, NTYPE, WCOL])
        x_sb = sb("x_sb", [P, B, NTT, D])
        up_sb = sb("up_sb", [P, K2, D])
        down_sb = sb("down_sb", [P, K2, D])
        wx_sb = sb("wx_sb", [P, K2, D])
        wh_sb = sb("wh_sb", [P, K2, D])
        b_rows = sb("b_rows", [NPART, D])

        zeros = sb("zeros", [P, P])
        ident = sb("ident", [P, P])
        sel3 = sb("sel3", [P, P // RANK, RANK])
        rmask = sb("rmask", [P, RANK])
        bmask = sb("bmask", [P, B])
        ones = sb("ones", [NPART, TC // 2], BF16)

        stats = sb("stats", [B, 6])
        mv = sb("mv", [B, 2])
        std = sb("std", [B, 1])
        rstd = sb("rstd", [B, 1])
        cn = sb("cn", [B, D])
        eps_sb = sb("eps_sb", [B, 1])
        cT = sb("cT", [P, K2, B])
        gT = sb("gT", [P, K2, B])
        gRep = sb("gRep", [P, K2, B, RANK])
        bmul = sb("bmul", [P, WCOL])
        bias_f = sb("bias_f", [P, D])
        wmul = sb("wmul", [P, 2, CH])
        fac = sb("fac", [P, D])
        facm = sb("facm", [P, B, D])
        b1m = sb("b1m", [Q, B, D])
        b2s = sb("b2s", [P, D])
        upT = sb("upT", [P, K2, D])
        wd = sb("wd", [P, B, K2, D])
        wu = sb("wu", [P, B, K2, D])

        xT = sb("xT", [P, K2, B, T])
        midT = sb("midT", [P, 2, K2, T])
        x2T = sb("x2T", [P, K2, T * B])

        whp = [sb(f"whp{i}", [P, K2, D], BF16) for i in range(NPART)]
        wxp = [sb(f"wxp{i}", [P, K2, D], BF16) for i in range(NPART)]
        wres = sb("wres", [P, 2, K2, D])
        b_part = sb("b_part", [NPART, 2, D], BF16)
        b_res = sb("b_res", [NPART, 2, D])
        b3 = sb("b3", [NPART, D])
        b3h = sb("b3h", [NPART, D], BF16)
        xp = [sb(f"xp{i}", [P, K2, TC], BF16) for i in range(NPART)]
        x_res = sb("x_res", [P, K2, TC])
        h_ring = sb("h_ring", [P, K2, PAIR, B])
        r_ring = sb("r_ring", [P, K2, 2, B])
        l_ring = sb("l_ring", [P, K2, 2, B], BF16)
        y_sb = sb("y_sb", [P, K2, B, PAIR])
        o_sb = sb("o_sb", [P, D])
        h_hi = h_ring[:].bitcast(BF16).rearrange("p k s (b w) -> p k s b w", w=2)[:, :, :, :, 1]
        r_hi = r_ring[:].bitcast(BF16).rearrange("p k s (b w) -> p k s b w", w=2)[:, :, :, :, 1]

        ld_cond = sem("ld_cond")
        ld_bias2 = sem("ld_bias2")
        ld_x = [sem(f"ld_x{b}") for b in range(B)]
        ld_base = sem("ld_base")
        ld_w2 = [sem(f"ld_w2_{c}") for c in range(NCH)]
        ld_rnn = sem("ld_rnn")
        const_ready = sem("const_ready")
        pool_step = sem("pool_step")
        dve_step = sem("dve_step")
        var_ready = sem("var_ready")
        std_ready = sem("std_ready")
        cn_ready = sem("cn_ready")
        condT_ready = sem("condT_ready")
        cT_psum = sem("cT_psum")
        cT_ready = sem("cT_ready")
        hpre_ready = sem("hpre_ready")
        g_ready = sem("g_ready")
        grep_ready = sem("grep_ready")
        tr_ready = sem("tr_ready")
        tr_dve = sem("tr_dve")
        tr_act = sem("tr_act")
        w_ready = sem("w_ready")
        facm_ready = sem("facm_ready")
        b1_ready = sem("b1_ready")
        b2_ready = sem("b2_ready")
        wd_psum = sem("wd_psum")
        wd_ready = sem("wd_ready")
        wu_psum = sem("wu_psum")
        wu_ready = sem("wu_ready")
        mid_psum = sem("mid_psum")
        mid_ready = sem("mid_ready")
        up_psum = sem("up_psum")
        x2_ready = sem("x2_ready")
        whp_ready = sem("whp_ready")
        wxp_ready = sem("wxp_ready")
        bp_ready = sem("bp_ready")
        xp1_ready = sem("xp1_ready")
        xr_ready = sem("xr_ready")
        xp2_ready = sem("xp2_ready")
        xp3_ready = sem("xp3_ready")
        h_ready = sem("h_ready")
        r_ready = sem("r_ready")
        l_ready = sem("l_ready")
        z_ready = sem("z_ready")
        y_ready = sem("y_ready")
        yT_ready = sem("yT_ready")
        o_ready = sem("o_ready")
        out_done = sem("out_done")

        block = ctx.enter_context(nc.Block())

        NTR = B * K2 + 1

        def tr_bank(g):
            return bank[4 + g % 3]

        def slot_before(s):
            return (s - 1) % PAIR

        SUMS, TURN, ROWS, PREFETCH = 3, 5, 5, 8

        def zbank(p, q, m):
            return bank[4 * p + 2 * q + m]

        def over_pairs(eng, body):
            body(0, True, False)
            body(1, False, False)
            with eng.Fori(2, NPAIR - 1) as pair:
                body(pair, False, False)
            body(NPAIR - 1, False, True)

        @block.sync
        def _(sp):
            sp.dma_start(cond_sb[:], cond).then_inc(ld_cond, 16)
            sp.dma_start(gamma_sb[:], ln_gamma.partition_broadcast(B)).then_inc(ld_cond, 16)
            sp.dma_start(beta_sb[:], ln_beta.partition_broadcast(B)).then_inc(ld_cond, 16)
            sp.dma_start(w1_sb[:], W1.rearrange("(k p) n -> p k n", p=P)).then_inc(ld_cond, 16)
            sp.dma_start(bias1_sb[:], bias1.rearrange("(k p) -> p k", p=P),
                         allow_slow_non_contiguous=True).then_inc(ld_cond, 16)
            for j in range(NTYPE):
                sp.dma_start(bias2_sb[Q * j:Q * (j + 1), :],
                             bias2[WCOL * j:WCOL * (j + 1)].partition_broadcast(Q)).then_inc(ld_bias2, 16)
            for b in range(B):
                sp.dma_start(x_sb[:, b], x[b].rearrange("(n p) d -> p n d", p=P)).then_inc(ld_x[b], 16)
            sp.dma_start(up_sb[:], base_up.rearrange("(k p) n -> p k n", p=P)).then_inc(ld_base, 16)
            sp.dma_start(down_sb[:], base_down.rearrange("(k p) n -> p k n", p=P)).then_inc(ld_base, 16)
            w2v = W2.rearrange("(k p) (j n) -> k p j n", p=P, j=NTYPE)
            for c in range(NCH):
                for k in range(K2):
                    sp.dma_start(w2_sb[:, k, :, CH * c:CH * (c + 1)],
                                 w2v[k, :, :, CH * c:CH * (c + 1)]).then_inc(ld_w2[c], 16)
            sp.dma_start(wh_sb[:], Wh.rearrange("(k p) n -> p k n", p=P)).then_inc(ld_rnn, 16)
            sp.dma_start(wx_sb[:], Wx.rearrange("(k p) n -> p k n", p=P)).then_inc(ld_rnn, 16)
            sp.dma_start(b_rows[:], b_rnn.partition_broadcast(NPART)).then_inc(ld_rnn, 16)

            def write_pair(done_pair):
                sp.wait_ge(o_ready, done_pair + 1)
                for b in range(B):
                    sp.dma_start(out[b, bass.ds(done_pair * PAIR, PAIR), :],
                                 o_sb[PAIR * b:PAIR * (b + 1), :]).then_inc(out_done, 16)

            def output(pair, first, last):
                if not first:
                    write_pair(pair - 1)
                if last:
                    write_pair(pair)

            over_pairs(sp, output)
            sp.wait_ge(out_done, 16 * B * NPAIR)

        @block.gpsimd
        def _(pool):
            nc.gpsimd.memset(zeros[:], 0.0).then_inc(pool_step, 1)
            nc.gpsimd.memset(ones[:], 1.0).then_inc(const_ready, 1)
            nc.gpsimd.memset(eps_sb[:], LN_EPS).then_inc(const_ready, 1)
            pool.wait_ge(pool_step, 1)
            nc.gpsimd.affine_select(out=ident[:], in_=zeros[:], compare_op=ALU.not_equal, fill=1.0, base=0,
                                    pattern=[[-1, P]], channel_multiplier=1).then_inc(const_ready, 1)
            nc.gpsimd.affine_select(out=sel3[:].rearrange("p q r -> p (q r)"), in_=zeros[:],
                                    compare_op=ALU.not_equal, fill=1.0, base=0,
                                    pattern=[[-RANK, P // RANK], [-1, RANK]],
                                    channel_multiplier=1).then_inc(const_ready, 1)
            count = [1]

            def then_wait(ins):
                count[0] += 1
                ins.then_inc(pool_step, 1)
                pool.wait_ge(pool_step, count[0])

            def parts(src, dst):
                then_wait(nc.gpsimd.tensor_copy(dst[0][:], src[:]))
                then_wait(nc.gpsimd.tensor_tensor(wres[:, 0], src[:], dst[0][:], ALU.subtract))
                then_wait(nc.gpsimd.tensor_copy(dst[1][:], wres[:, 0]))
                then_wait(nc.gpsimd.tensor_tensor(wres[:, 1], wres[:, 0], dst[1][:], ALU.subtract))
                return nc.gpsimd.tensor_copy(dst[2][:], wres[:, 1])

            pool.wait_ge(ld_rnn, 48)
            parts(wx_sb, wxp).then_inc(wxp_ready, 1)
            pool.wait_ge(wxp_ready, 1)
            parts(wh_sb, whp).then_inc(whp_ready, 1)

        @block.scalar
        def _(act):
            act.wait_ge(var_ready, 1)
            act.wait_ge(const_ready, 4)
            nc.scalar.activation(std[:], mv[:, 1:2], ACT.Sqrt, bias=eps_sb[:]).then_inc(std_ready, 1)
            act.wait_ge(condT_ready, 1)
            for m in range(K2):
                nc.scalar.copy(h_ring[:, m, PAIR - 1, :], bank[7][:, B * m:B * (m + 1)]).then_inc(h_ready, 1)

            def move_transposes(g):
                act.wait_ge(tr_ready, g + 1)
                nc.scalar.copy(xT[:, g % K2, g // K2, :], tr_bank(g)[:]).then_inc(tr_act, 1)

            move_transposes(1)
            act.wait_ge(hpre_ready, 1)
            for m in range(K2):
                nc.scalar.activation(gT[:, m, :], bank[7][:, 32 + B * m:32 + B * (m + 1)], ACT.Gelu,
                                     bias=bias1_sb[:, m:m + 1]).then_inc(g_ready, 1)
            for g in range(3, B * K2, 2):
                move_transposes(g)
            act.wait_ge(facm_ready, 1)
            nc.scalar.copy(b1m[:], facm[Q * B1:Q * (B1 + 1)]).then_inc(b1_ready, 1)
            for b in range(B):
                for m in range(K2):
                    act.wait_ge(mid_psum, K2 * b + m + 1)
                    if b >= 2 and m == 0:
                        act.wait_ge(up_psum, K2 * (b - 1))
                    nc.scalar.activation(midT[:, b % 2, m, :], bank[4 + 2 * (b % 2) + m][:],
                                         ACT.Gelu).then_inc(mid_ready, 1)

            def x_part1(col0):
                nc.scalar.copy(xp[0][:], x2T[:, :, bass.ds(col0, TC)]).then_inc(xp1_ready, 1)

            def x_part2(tile_no):
                act.wait_ge(xr_ready, tile_no + 1)
                nc.scalar.copy(xp[1][:], x_res[:]).then_inc(xp2_ready, 1)

            act.wait_ge(x2_ready, K2 * B)
            x_part1(0)
            x_part2(0)

            def move_rows(done_pair):
                act.wait_ge(yT_ready, done_pair + 1)
                if not (isinstance(done_pair, int) and done_pair == 0):
                    act.wait_ge(out_done, 16 * B * done_pair)
                nc.scalar.copy(o_sb[:], zbank(1, 0, 0)[:, 0:D]).then_inc(o_ready, 1)

            def states(pair, first, last):
                for s in range(PAIR):
                    if s % TS == 0 and not first:
                        act.wait_ge(y_ready, 2 * pair + s // TS - 1)
                    for m in range(K2):
                        act.wait_ge(z_ready, 2 * PAIR * pair + 2 * s + m + 1)
                        zt = zbank(s // TS, s % 2, m)[:, B * (s % TS // 2):B * (s % TS // 2 + 1)]
                        nc.scalar.activation(h_ring[:, m, s, :], zt, ACT.Tanh).then_inc(h_ready, 1)
                    if not (last and s >= TS):
                        if s % TS == 0:
                            x_part1((PAIR * pair + TS * (s // TS + 1)) * B)
                        if s % TS == 1:
                            x_part2(2 * pair + s // TS + 1)
                    if s == ROWS and not first:
                        move_rows(pair - 1)
                if last:
                    move_rows(pair)

            over_pairs(act, states)

        @block.vector
        def _(dve):
            steps = [0]

            def then_wait(ins):
                steps[0] += 1
                ins.then_inc(dve_step, 1)
                dve.wait_ge(dve_step, steps[0])

            dve.wait_ge(ld_cond, 80)
            then_wait(nc.vector.bn_stats(stats[:], cond_sb[:]))
            nc.vector.bn_aggr(mv[:], stats[:]).then_inc(var_ready, 1)
            dve.wait_ge(std_ready, 1)
            then_wait(nc.vector.reciprocal(rstd[:], std[:]))
            then_wait(nc.vector.tensor_scalar(cn[:], cond_sb[:], mv[:, 0:1], rstd[:], ALU.subtract, ALU.mult))
            then_wait(nc.vector.tensor_tensor(cn[:], cn[:], gamma_sb[:], ALU.mult))
            nc.vector.tensor_tensor(cn[:], cn[:], beta_sb[:], ALU.add).then_inc(cn_ready, 1)
            dve.wait_ge(const_ready, 4)
            nc.vector.tensor_reduce(rmask[:], sel3[:].rearrange("p q r -> p r q"), AX.X, ALU.add)
            then_wait(nc.vector.tensor_reduce(bmask[:], sel3[:].rearrange("p (j b) r -> p b j r", b=B), AX.XY,
                                              ALU.add))
            dve.wait_ge(cT_psum, 1)
            nc.vector.tensor_copy(cT[:].rearrange("p k b -> p (k b)"),
                                  bank[7][:, 16:16 + K2 * B]).then_inc(cT_ready, 1)

            def move_transposes(g):
                dve.wait_ge(tr_ready, g + 1)
                dst = xT[:, g % K2, g // K2, :] if g < B * K2 else upT[:].rearrange("p k n -> p (k n)")
                nc.vector.tensor_copy(dst, tr_bank(g)[:]).then_inc(tr_dve, 1)

            move_transposes(0)
            dve.wait_ge(g_ready, 2)
            nc.vector.tensor_copy(gRep[:], gT[:].unsqueeze(3).broadcast_to([P, K2, B, RANK])).then_inc(grep_ready, 1)
            for g in range(2, NTR, 2):
                move_transposes(g)

            def keep_rank(dst, src, tmp, n, srcsem=None):
                mask = rmask[:].unsqueeze(1).broadcast_to([P, n, RANK])
                then_wait(nc.vector.tensor_tensor(tmp.rearrange("p (d r) -> p d r", r=RANK),
                                                  src.rearrange("p (d r) -> p d r", r=RANK), mask, ALU.mult))
                then_wait(nc.vector.tensor_reduce(dst, tmp.rearrange("p (d r) -> p d r", r=RANK), AX.X, ALU.add))

            dve.wait_ge(ld_bias2, 64)
            keep_rank(bias_f[:], bias2_sb[:], bmul[:], D)
            DC = CH // RANK
            for c in range(NCH):
                dve.wait_ge(w_ready, c + 1)
                keep_rank(fac[:, DC * c:DC * (c + 1)], bank[c][:], wmul[:, c % 2], DC)
            then_wait(nc.vector.tensor_tensor(fac[:], fac[:], bias_f[:], ALU.add))
            nc.vector.tensor_copy(b2s[Q * A2:Q * (A2 + 1)], fac[Q * B2:Q * (B2 + 1)]).then_inc(b2_ready, 1)
            nc.vector.tensor_tensor(facm[:], fac[:].unsqueeze(1).broadcast_to([P, B, D]),
                                    bmask[:].unsqueeze(2).broadcast_to([P, B, D]), ALU.mult).then_inc(facm_ready, 1)
            dve.wait_ge(ld_base, 32)
            for b in range(B):
                dve.wait_ge(wd_psum, b + 1)
                nc.vector.tensor_tensor(wd[:, b].rearrange("p k n -> p (k n)"), bank[4 + b][:],
                                        down_sb[:].rearrange("p k n -> p (k n)"), ALU.add).then_inc(wd_ready, 1)
            for b in range(B):
                dve.wait_ge(wu_psum, b + 1)
                nc.vector.tensor_tensor(wu[:, b].rearrange("p k n -> p (k n)"), bank[b][:],
                                        upT[:].rearrange("p k n -> p (k n)"), ALU.add).then_inc(wu_ready, 1)
            for b in range(B):
                for n in range(K2):
                    dve.wait_ge(up_psum, K2 * b + n + 1)
                    nc.vector.scalar_tensor_tensor(
                        out=x2T[:, n].rearrange("p (t b) -> p b t", b=B)[:, b], in0=xT[:, n, b, :], scalar=2.0,
                        in1=bank[2 * (b % 2) + n][:], op0=ALU.mult, op1=ALU.add).then_inc(x2_ready, 1)

            def x_res1(tile_no, col0):
                dve.wait_ge(xp1_ready, tile_no + 1)
                nc.vector.tensor_tensor(x_res[:], x2T[:, :, bass.ds(col0, TC)], xp[0][:],
                                        ALU.subtract).then_inc(xr_ready, 1)

            def x_part3(tile_no):
                dve.wait_ge(xp2_ready, tile_no + 1)
                nc.vector.tensor_tensor(xp[2][:], x_res[:], xp[1][:], ALU.subtract).then_inc(xp3_ready, 1)

            x_res1(0, 0)
            dve.wait_ge(ld_rnn, 48)
            then_wait(nc.vector.tensor_copy(b_part[:, 0], b_rows[:]))
            then_wait(nc.vector.tensor_tensor(b_res[:, 0], b_rows[:], b_part[:, 0], ALU.subtract))
            then_wait(nc.vector.tensor_copy(b_part[:, 1], b_res[:, 0]))
            then_wait(nc.vector.tensor_tensor(b_res[:, 1], b_res[:, 0], b_part[:, 1], ALU.subtract))
            then_wait(nc.vector.tensor_scalar(b3[:], b_part[:, 0], ident[0:NPART, 0:1], None, ALU.mult))
            then_wait(nc.vector.scalar_tensor_tensor(out=b3[:], in0=b_part[:, 1], scalar=ident[0:NPART, 1:2],
                                                     in1=b3[:], op0=ALU.mult, op1=ALU.add))
            nc.vector.scalar_tensor_tensor(out=b3h[:], in0=b_res[:, 1], scalar=ident[0:NPART, 2:3],
                                           in1=b3[:], op0=ALU.mult, op1=ALU.add).then_inc(bp_ready, 1)
            x_part3(0)

            def output_sum(p, col0, in_pair):
                if p == 0 and not (isinstance(in_pair, int) and in_pair == 0):
                    dve.wait_ge(yT_ready, in_pair)
                for k in range(K2):
                    last = nc.vector.tensor_tensor(
                        y_sb[:, k, :, TS * p:TS * (p + 1)],
                        x2T[:, k, bass.ds(col0, TC)].rearrange("p (t b) -> p b t", b=B),
                        h_ring[:, k, TS * p:TS * (p + 1), :].rearrange("p t b -> p b t"), ALU.add)
                last.then_inc(y_ready, 1)

            def residues(pair, first, last):
                for s in range(PAIR):
                    q = s % 2
                    before = slot_before(s)
                    for k in range(K2):
                        dve.wait_ge(h_ready, 2 * PAIR * pair + 2 * s + k + 1)
                        nc.vector.tensor_tensor(r_ring[:, k, q, :], h_ring[:, k, before, :], h_hi[:, k, before, :],
                                                ALU.subtract).then_inc(r_ready, 1)
                    for k in range(K2):
                        dve.wait_ge(r_ready, 2 * PAIR * pair + 2 * s + k + 1)
                        nc.vector.tensor_tensor(l_ring[:, k, q, :], r_ring[:, k, q, :], r_hi[:, k, q, :],
                                                ALU.subtract).then_inc(l_ready, 1)
                    if not (last and s >= TS):
                        if s % TS == 1:
                            x_res1(2 * pair + s // TS + 1, (PAIR * pair + TS * (s // TS + 1)) * B)
                        if s % TS == 2:
                            x_part3(2 * pair + s // TS + 1)
                    if s == SUMS and not first:
                        output_sum(1, (PAIR * pair - TS) * B, pair - 1)
                    if s == TS + SUMS:
                        output_sum(0, PAIR * pair * B, pair)
                if last:
                    dve.wait_ge(h_ready, 2 * PAIR * (pair + 1) + 2)
                    output_sum(1, (PAIR * pair + TS) * B, pair)

            over_pairs(dve, residues)

        @block.tensor
        def _(pe):
            pe.wait_ge(const_ready, 4)
            pe.wait_ge(ld_cond, 80)
            for k in range(K2):
                last = nc.tensor.transpose(bank[7][:, B * k:B * (k + 1)], cond_sb[:, P * k:P * (k + 1)],
                                           ident[0:B, 0:B])
            last.then_inc(condT_ready, 1)

            def transposes(g):
                if g >= 3:
                    prev = g - 3
                    pe.wait_ge(tr_dve if prev % 2 == 0 else tr_act, prev // 2 + 1)
                for i in range(4):
                    if g < B * K2:
                        src = x_sb[:, g // K2, i, P * (g % K2):P * (g % K2 + 1)]
                    else:
                        src = up_sb[:, i % 2, P * (i // 2):P * (i // 2 + 1)]
                    last = nc.tensor.transpose(tr_bank(g)[:, P * i:P * (i + 1)], src, ident[:])
                last.then_inc(tr_ready, 1)

            pe.wait_ge(cn_ready, 1)
            pe.wait_ge(h_ready, 2)
            for k in range(K2):
                last = nc.tensor.transpose(bank[7][:, 16 + B * k:16 + B * (k + 1)], cn[:, P * k:P * (k + 1)],
                                           ident[0:B, 0:B])
            last.then_inc(cT_psum, 1)
            pe.wait_ge(ld_x[0], 16)
            transposes(0)
            transposes(1)
            pe.wait_ge(cT_ready, 1)
            for m in range(K2):
                for k in range(K2):
                    last = nc.tensor.matmul(bank[7][:, 32 + B * m:32 + B * (m + 1)], w1_sb[:, k, P * m:P * (m + 1)],
                                            cT[:, k, :], start=(k == 0), stop=(k == K2 - 1))
            last.then_inc(hpre_ready, 1)
            for g in range(2, NTR):
                if g < B * K2 and g % K2 == 0:
                    pe.wait_ge(ld_x[g // K2], 16)
                if g == B * K2:
                    pe.wait_ge(ld_base, 32)
                transposes(g)
            pe.wait_ge(grep_ready, 1)
            for c in range(NCH):
                pe.wait_ge(ld_w2[c], 32)
                for k in range(K2):
                    for j in range(NTYPE):
                        last = nc.tensor.matmul(bank[c][Q * j:Q * (j + 1), :],
                                                gRep[:, k].rearrange("p b r -> p (b r)"),
                                                w2_sb[:, k, j, CH * c:CH * (c + 1)], start=(k == 0),
                                                stop=(k == K2 - 1))
                last.then_inc(w_ready, 1)
            pe.wait_ge(b2_ready, 1)
            pe.wait_ge(facm_ready, 1)
            pe.wait_ge(tr_dve, NTR // 2 + 1)
            pe.wait_ge(tr_act, B * K2 // 2)

            def low_down(b):
                for k in range(K2):
                    last = nc.tensor.matmul(bank[4 + b][:, D * k:D * (k + 1)],
                                            facm[Q * A2:Q * (A2 + 1), b, P * k:P * (k + 1)],
                                            b2s[Q * A2:Q * (A2 + 1), :], start=True, stop=True)
                last.then_inc(wd_psum, 1)

            def low_up(b):
                for k in range(K2):
                    last = nc.tensor.matmul(bank[b][:, D * k:D * (k + 1)], b1m[:, b, P * k:P * (k + 1)],
                                            fac[Q * A1:Q * (A1 + 1), :], start=True, stop=True)
                last.then_inc(wu_psum, 1)

            def down(b):
                pe.wait_ge(wd_ready, 2 if b == 0 else B)
                if b >= 2:
                    pe.wait_ge(mid_ready, K2 * (b - 1))
                for m in range(K2):
                    for k in range(K2):
                        last = nc.tensor.matmul(bank[4 + 2 * (b % 2) + m][:], wd[:, b, k, P * m:P * (m + 1)],
                                                xT[:, k, b, :], start=(k == 0), stop=(k == K2 - 1))
                    last.then_inc(mid_psum, 1)

            def up(b):
                pe.wait_ge(mid_ready, K2 * (b + 1))
                pe.wait_ge(wu_ready, 2 if b == 0 else B)
                if b >= 2:
                    pe.wait_ge(x2_ready, K2 * (b - 1))
                for n in range(K2):
                    for k in range(K2):
                        last = nc.tensor.matmul(bank[2 * (b % 2) + n][:], wu[:, b, k, P * n:P * (n + 1)],
                                                midT[:, b % 2, k, :], start=(k == 0), stop=(k == K2 - 1))
                    last.then_inc(up_psum, 1)

            for b in range(B):
                low_down(b)
            pe.wait_ge(b1_ready, 1)
            down(0)
            low_up(0)
            low_up(1)
            down(1)
            low_up(2)
            low_up(3)
            up(0)
            for b in range(2, B):
                down(b)
                up(b - 1)
            up(B - 1)

            PAIRS6 = [(0, 0), (1, 0), (2, 0), (0, 1), (1, 1), (0, 2)]

            def input_products(p, q, m, half=None):
                zb = zbank(p, q, m)[:, 0:TC // 2]
                if half != 1:
                    nc.tensor.matmul(zb, b3h[:, P * m:P * (m + 1)], ones[:], start=True, stop=False,
                                     skip_group_check=True)
                for k in range(K2) if half is None else (half,):
                    for w, v in PAIRS6:
                        rhs = xp[v][:, k].rearrange("p (t q b) -> p t q b", q=2, b=B)[:, :, q, :]
                        nc.tensor.matmul(zb, wxp[w][:, k, P * m:P * (m + 1)], rhs, start=False, stop=False,
                                         skip_group_check=True)

            def output_transposes(done_pair):
                pe.wait_ge(y_ready, 2 * done_pair + 2)
                if not (isinstance(done_pair, int) and done_pair == 0):
                    pe.wait_ge(o_ready, done_pair)
                for n in range(K2):
                    last = nc.tensor.transpose(zbank(1, 0, 0)[:, P * n:P * (n + 1)],
                                               y_sb[:, n].rearrange("p b t -> p (b t)"), ident[:])
                last.then_inc(yT_ready, 1)

            def recurrence(pair, first, last):
                for s in range(PAIR):
                    p, q, before = s // TS, s % 2, slot_before(s)
                    cols = slice(B * (s % TS // 2), B * (s % TS // 2 + 1))
                    done = 2 * PAIR * pair + 2 * s

                    def product(part, k, m, rhs, stop=False):
                        return nc.tensor.matmul(zbank(p, q, m)[:, cols], whp[part][:, k, P * m:P * (m + 1)], rhs,
                                                start=False, stop=stop, skip_group_check=True)

                    for k in range(K2):
                        pe.wait_ge(h_ready, done + k + 1)
                        for m in range(K2):
                            for part in range(NPART):
                                product(part, k, m, h_hi[:, k, before, :])
                    pe.wait_ge(r_ready, done + 1)
                    for m in range(K2):
                        for part in range(2):
                            product(part, 0, m, r_hi[:, 0, q, :])
                    pe.wait_ge(r_ready, done + 2)
                    for part in range(2):
                        product(part, 1, 0, r_hi[:, 1, q, :])
                    pe.wait_ge(l_ready, done + 1)
                    product(0, 0, 0, l_ring[:, 0, q, :])
                    pe.wait_ge(l_ready, done + 2)
                    product(0, 1, 0, l_ring[:, 1, q, :], stop=True).then_inc(z_ready, 1)
                    for part in range(2):
                        product(part, 1, 1, r_hi[:, 1, q, :])
                    product(0, 0, 1, l_ring[:, 0, q, :])
                    product(0, 1, 1, l_ring[:, 1, q, :], stop=True).then_inc(z_ready, 1)

                    if s == TURN and not first:
                        output_transposes(pair - 1)
                    i = s % TS - PREFETCH
                    if i >= 0 and not (last and p == 1):
                        if i == 0:
                            pe.wait_ge(xp2_ready, 2 * pair + p + 2)
                            pe.wait_ge(xp3_ready, 2 * pair + p + 2)
                            if p == 0 and not first:
                                pe.wait_ge(o_ready, pair)
                        input_products(1 - p, i // 4, i // 2 % 2, i % 2)
                if last:
                    output_transposes(pair)

            pe.wait_ge(wxp_ready, 1)
            pe.wait_ge(bp_ready, 1)
            pe.wait_ge(xp2_ready, 1)
            pe.wait_ge(xp3_ready, 1)
            for q in range(2):
                for m in range(K2):
                    input_products(0, q, m)
            pe.wait_ge(whp_ready, 1)
            over_pairs(pe, recurrence)


_INS = ["x", "cond_1024", "L0_cond_base_up", "L0_cond_base_down", "L0_cond_ln_gamma", "L0_cond_ln_beta",
        "L0_cond_W1", "L0_cond_bias1", "L0_cond_W2", "L0_cond_bias2", "L1_cond_Wx", "L1_cond_Wh", "L1_cond_b"]


def kernel(**inputs):
    import numpy as _np
    import concourse.bacc as _bacc
    from concourse import mybir as _mybir
    from concourse.bass_utils import run_bass_kernel_spmd as _run

    nc = _bacc.Bacc("TRN2", target_bir_lowering=False, num_devices=1)
    arrays, args = {}, []
    for name in _INS:
        a = _np.ascontiguousarray(inputs[name])
        arrays[f"in_{name}"] = a
        args.append(nc.dram_tensor(f"in_{name}", a.shape, _mybir.dt.from_np(a.dtype), kind="ExternalInput").ap())
    shape = inputs["x"].shape
    args.append(nc.dram_tensor("out_0", shape, _mybir.dt.float32, kind="ExternalOutput").ap())
    adaptive_lowrank_then_recurrence(nc, *args)
    r = _run(nc, [arrays], core_ids=[0])
    return r.results[0]["out_0"]
```

```python
from contextlib import ExitStack

import concourse.bass as bass
from concourse import mybir

F32 = mybir.dt.float32
BF16 = mybir.dt.bfloat16
ALU = mybir.AluOpType
ACT = mybir.ActivationFunctionType
AX = mybir.AxisListType

P = 128
RANK = 8
LN_EPS = 1e-5
TS = 16
PAIR = 2 * TS
NPART = 3


def adaptive_lowrank_then_recurrence(nc, x, cond, base_up, base_down, ln_gamma, ln_beta, W1, bias1, W2,
                                     bias2, Wx, Wh, b_rnn, out):
    B, T, D = x.shape
    K2 = D // P
    NTYPE = 4
    A1, B1, A2, B2 = range(NTYPE)
    Q = B * RANK
    WCOL = D * RANK
    CH = 512
    NCH = WCOL // CH
    NTT = T // P
    NTILE = T // TS
    NPAIR = NTILE // 2
    TC = TS * B
    assert B * PAIR == P
    assert Q == 32 and K2 == 2 and D == 256 and T == 512 and NCH == 4

    with ExitStack() as ctx:
        def sb(name, shape, dt=F32):
            return ctx.enter_context(nc.sbuf_tensor(name, shape, dt))

        def sem(name):
            return ctx.enter_context(nc.semaphore(name))

        bank = [ctx.enter_context(nc.psum_tensor(f"bank{i}", [P, 512], F32)) for i in range(8)]

        cond_sb = sb("cond_sb", [B, D])
        gamma_sb = sb("gamma_sb", [B, D])
        beta_sb = sb("beta_sb", [B, D])
        w1_sb = sb("w1_sb", [P, K2, D])
        bias1_sb = sb("bias1_sb", [P, K2])
        bias2_sb = sb("bias2_sb", [NTYPE, WCOL])
        w2_sb = sb("w2_sb", [P, K2, NTYPE, WCOL])
        x_sb = sb("x_sb", [P, B, NTT, D])
        up_sb = sb("up_sb", [P, K2, D])
        down_sb = sb("down_sb", [P, K2, D])
        wx_sb = sb("wx_sb", [P, K2, D])
        wh_sb = sb("wh_sb", [P, K2, D])
        b_rows = sb("b_rows", [NPART, D])

        zeros = sb("zeros", [P, P])
        ident = sb("ident", [P, P])
        sel3 = sb("sel3", [P, P // RANK, RANK])
        rmask = sb("rmask", [P, RANK])
        bmask = sb("bmask", [P, B])
        quadrant = sb("quadrant", [NTYPE, NTYPE, Q])
        ones = sb("ones", [NPART, TC // 2], BF16)

        stats = sb("stats", [B, 6])
        mv = sb("mv", [B, 2])
        std = sb("std", [B, 1])
        rstd = sb("rstd", [B, 1])
        cn = sb("cn", [B, D])
        eps_sb = sb("eps_sb", [B, 1])
        cT = sb("cT", [P, K2, B])
        gT = sb("gT", [P, K2, B])
        gRep = sb("gRep", [P, K2, B, RANK])
        wmul = sb("wmul", [P, 2, CH])
        fac = sb("fac", [P, D])
        facm = sb("facm", [P, B, D])
        b1m = sb("b1m", [Q, B, D])
        b2s = sb("b2s", [P, D])
        upT = sb("upT", [P, K2, D])
        wd = sb("wd", [P, B, K2, D])
        wu = sb("wu", [P, B, K2, D])

        xT = sb("xT", [P, K2, B, T])
        midT = sb("midT", [P, 2, K2, T])
        x2T = sb("x2T", [P, K2, T * B])

        whp = [sb(f"whp{i}", [P, K2, D], BF16) for i in range(NPART)]
        wxp = [sb(f"wxp{i}", [P, K2, D], BF16) for i in range(NPART)]
        wres = sb("wres", [P, 2, K2, D])
        b_part = sb("b_part", [NPART, 2, D], BF16)
        b_res = sb("b_res", [NPART, 2, D])
        b3 = sb("b3", [NPART, NPART, D])
        b3h = sb("b3h", [NPART, D], BF16)
        xp = [sb(f"xp{i}", [P, K2, TC], BF16) for i in range(NPART)]
        x_res = sb("x_res", [P, K2, TC])
        h_ring = sb("h_ring", [P, K2, PAIR, B])
        r_ring = sb("r_ring", [P, K2, 2, B])
        l_ring = sb("l_ring", [P, K2, 2, B], BF16)
        y_sb = sb("y_sb", [P, K2, B, PAIR])
        o_sb = sb("o_sb", [P, D])
        h_hi = h_ring[:].bitcast(BF16).rearrange("p k s (b w) -> p k s b w", w=2)[:, :, :, :, 1]
        r_hi = r_ring[:].bitcast(BF16).rearrange("p k s (b w) -> p k s b w", w=2)[:, :, :, :, 1]

        ld_cond = sem("ld_cond")
        ld_bias2 = sem("ld_bias2")
        ld_x = [sem(f"ld_x{b}") for b in range(B)]
        ld_base = sem("ld_base")
        ld_w2 = [[sem(f"ld_w2_{c}_{k}") for k in range(K2)] for c in range(NCH)]
        ld_rnn = sem("ld_rnn")
        const_ready = sem("const_ready")
        pool_step = sem("pool_step")
        dve_step = sem("dve_step")
        quadrant_ready = sem("quadrant_ready")
        var_ready = sem("var_ready")
        std_ready = sem("std_ready")
        cn_ready = sem("cn_ready")
        condT_ready = sem("condT_ready")
        cT_psum = sem("cT_psum")
        cT_ready = sem("cT_ready")
        hpre_ready = sem("hpre_ready")
        g_ready = sem("g_ready")
        grep_ready = sem("grep_ready")
        tr_ready = sem("tr_ready")
        tr_moved = sem("tr_moved")
        upT_psum = sem("upT_psum")
        upT_ready = sem("upT_ready")
        ld_up = sem("ld_up")
        w_ready = sem("w_ready")
        facm_ready = sem("facm_ready")
        b1_ready = sem("b1_ready")
        b2_ready = sem("b2_ready")
        wd_psum = sem("wd_psum")
        wd_ready = sem("wd_ready")
        wu_psum = sem("wu_psum")
        wu_ready = sem("wu_ready")
        mid_psum = sem("mid_psum")
        mid_ready = sem("mid_ready")
        up_psum = sem("up_psum")
        x2_ready = sem("x2_ready")
        whp_ready = sem("whp_ready")
        wxp_ready = sem("wxp_ready")
        bp_ready = sem("bp_ready")
        xp1_ready = sem("xp1_ready")
        xr_ready = sem("xr_ready")
        xp2_ready = sem("xp2_ready")
        xp3_ready = sem("xp3_ready")
        h_ready = sem("h_ready")
        r_ready = sem("r_ready")
        l_ready = sem("l_ready")
        z_ready = sem("z_ready")
        y_ready = sem("y_ready")
        yT_ready = sem("yT_ready")
        o_ready = sem("o_ready")
        out_done = sem("out_done")

        block = ctx.enter_context(nc.Block())

        def tr_bank(g):
            return bank[4 + g % 3]

        def slot_before(s):
            return (s - 1) % PAIR

        SUMS, TURN, ROWS, PREFETCH = 3, 4, 5, 8

        def zbank(p, q, m):
            return bank[4 * p + 2 * q + m]

        def over_pairs(eng, body):
            body(0, True, False)
            body(1, False, False)
            with eng.Fori(2, NPAIR - 1) as pair:
                body(pair, False, False)
            body(NPAIR - 1, False, True)

        @block.sync
        def _(sp):
            sp.dma_start(cond_sb[:], cond).then_inc(ld_cond, 16)
            sp.dma_start(gamma_sb[:], ln_gamma.partition_broadcast(B)).then_inc(ld_cond, 16)
            sp.dma_start(beta_sb[:], ln_beta.partition_broadcast(B)).then_inc(ld_cond, 16)
            sp.dma_start(w1_sb[:], W1.rearrange("(k p) n -> p k n", p=P)).then_inc(ld_cond, 16)
            sp.dma_start(bias1_sb[:], bias1.rearrange("(k p) -> p k", p=P),
                         allow_slow_non_contiguous=True).then_inc(ld_cond, 16)
            sp.dma_start(bias2_sb[:], bias2.rearrange("(j n) -> j n", j=NTYPE)).then_inc(ld_bias2, 16)
            sp.dma_start(up_sb[:], base_up.rearrange("(k p) n -> p k n", p=P)).then_inc(ld_up, 16)
            for b in range(B // 2):
                sp.dma_start(x_sb[:, b], x[b].rearrange("(n p) d -> p n d", p=P)).then_inc(ld_x[b], 16)
            w2v = W2.rearrange("(k p) (j n) -> k p j n", p=P, j=NTYPE)
            for c in range(NCH):
                for k in range(K2):
                    sp.dma_start(w2_sb[:, k, :, CH * c:CH * (c + 1)],
                                 w2v[k, :, :, CH * c:CH * (c + 1)]).then_inc(ld_w2[c][k], 16)
            for b in range(B // 2, B):
                sp.dma_start(x_sb[:, b], x[b].rearrange("(n p) d -> p n d", p=P)).then_inc(ld_x[b], 16)
            sp.dma_start(down_sb[:], base_down.rearrange("(k p) n -> p k n", p=P)).then_inc(ld_base, 16)
            sp.dma_start(wh_sb[:], Wh.rearrange("(k p) n -> p k n", p=P)).then_inc(ld_rnn, 16)
            sp.dma_start(wx_sb[:], Wx.rearrange("(k p) n -> p k n", p=P)).then_inc(ld_rnn, 16)
            sp.dma_start(b_rows[:], b_rnn.partition_broadcast(NPART)).then_inc(ld_rnn, 16)

            def write_pair(done_pair):
                sp.wait_ge(o_ready, done_pair + 1)
                for b in range(B):
                    sp.dma_start(out[b, bass.ds(done_pair * PAIR, PAIR), :],
                                 o_sb[PAIR * b:PAIR * (b + 1), :]).then_inc(out_done, 16)

            def output(pair, first, last):
                if not first:
                    write_pair(pair - 1)
                if last:
                    write_pair(pair)

            over_pairs(sp, output)
            sp.wait_ge(out_done, 16 * B * NPAIR)

        @block.gpsimd
        def _(pool):
            nc.gpsimd.memset(zeros[:], 0.0).then_inc(pool_step, 1)
            nc.gpsimd.memset(ones[:], 1.0).then_inc(const_ready, 1)
            nc.gpsimd.memset(eps_sb[:], LN_EPS).then_inc(const_ready, 1)
            pool.wait_ge(pool_step, 1)
            nc.gpsimd.affine_select(out=ident[:], in_=zeros[:], compare_op=ALU.not_equal, fill=1.0, base=0,
                                    pattern=[[-1, P]], channel_multiplier=1).then_inc(const_ready, 1)
            nc.gpsimd.affine_select(out=sel3[:].rearrange("p q r -> p (q r)"), in_=zeros[:],
                                    compare_op=ALU.not_equal, fill=1.0, base=0,
                                    pattern=[[-RANK, P // RANK], [-1, RANK]],
                                    channel_multiplier=1).then_inc(const_ready, 1)
            count = [1]

            def then_wait(ins):
                count[0] += 1
                ins.then_inc(pool_step, 1)
                pool.wait_ge(pool_step, count[0])

            def parts(src, dst):
                then_wait(nc.gpsimd.tensor_copy(dst[0][:], src[:]))
                then_wait(nc.gpsimd.tensor_tensor(wres[:, 0], src[:], dst[0][:], ALU.subtract))
                then_wait(nc.gpsimd.tensor_copy(dst[1][:], wres[:, 0]))
                then_wait(nc.gpsimd.tensor_tensor(wres[:, 1], wres[:, 0], dst[1][:], ALU.subtract))
                return nc.gpsimd.tensor_copy(dst[2][:], wres[:, 1])

            pool.wait_ge(ld_rnn, 48)
            parts(wx_sb, wxp).then_inc(wxp_ready, 1)
            pool.wait_ge(wxp_ready, 1)
            parts(wh_sb, whp).then_inc(whp_ready, 1)
            then_wait(nc.gpsimd.tensor_copy(b_part[:, 0], b_rows[:]))
            then_wait(nc.gpsimd.tensor_tensor(b_res[:, 0], b_rows[:], b_part[:, 0], ALU.subtract))
            then_wait(nc.gpsimd.tensor_copy(b_part[:, 1], b_res[:, 0]))
            then_wait(nc.gpsimd.tensor_tensor(b_res[:, 1], b_res[:, 0], b_part[:, 1], ALU.subtract))
            row = ident[0:NPART, 0:NPART]
            then_wait(nc.gpsimd.tensor_scalar(b3[:, 0], b_part[:, 0], row[:, 0:1], None, ALU.mult))
            then_wait(nc.gpsimd.tensor_scalar(b3[:, 1], b_part[:, 1], row[:, 1:2], None, ALU.mult))
            then_wait(nc.gpsimd.tensor_scalar(b3[:, 2], b_res[:, 1], row[:, 2:3], None, ALU.mult))
            then_wait(nc.gpsimd.tensor_tensor(b3[:, 0], b3[:, 0], b3[:, 1], ALU.add))
            nc.gpsimd.tensor_tensor(b3h[:], b3[:, 0], b3[:, 2], ALU.add).then_inc(bp_ready, 1)

        @block.scalar
        def _(act):
            act.wait_ge(var_ready, 1)
            act.wait_ge(const_ready, 4)
            nc.scalar.activation(std[:], mv[:, 1:2], ACT.Sqrt, bias=eps_sb[:]).then_inc(std_ready, 1)
            act.wait_ge(condT_ready, 1)
            for m in range(K2):
                nc.scalar.copy(h_ring[:, m, PAIR - 1, :], bank[7][:, B * m:B * (m + 1)]).then_inc(h_ready, 1)

            def move_transposes(g):
                act.wait_ge(tr_ready, g + 1)
                nc.scalar.copy(xT[:, g % K2, g // K2, :], tr_bank(g)[:]).then_inc(tr_moved, 1)

            act.wait_ge(hpre_ready, 1)
            for m in range(K2):
                nc.scalar.activation(gT[:, m, :], bank[7][:, 32 + B * m:32 + B * (m + 1)], ACT.Gelu,
                                     bias=bias1_sb[:, m:m + 1]).then_inc(g_ready, 1)
            for g in range(B * K2):
                move_transposes(g)
            act.wait_ge(facm_ready, 1)
            nc.scalar.copy(b1m[:], facm[Q * B1:Q * (B1 + 1)]).then_inc(b1_ready, 1)
            for b in range(B):
                for m in range(K2):
                    act.wait_ge(mid_psum, K2 * b + m + 1)
                    if b >= 2 and m == 0:
                        act.wait_ge(up_psum, K2 * (b - 1))
                    nc.scalar.activation(midT[:, b % 2, m, :], bank[4 + 2 * (b % 2) + m][:],
                                         ACT.Gelu).then_inc(mid_ready, 1)

            def x_part1(col0):
                nc.scalar.copy(xp[0][:], x2T[:, :, bass.ds(col0, TC)]).then_inc(xp1_ready, 1)

            def x_part2(tile_no):
                act.wait_ge(xr_ready, tile_no + 1)
                nc.scalar.copy(xp[1][:], x_res[:]).then_inc(xp2_ready, 1)

            act.wait_ge(x2_ready, K2 * B)
            x_part1(0)
            x_part2(0)

            def move_rows(done_pair):
                act.wait_ge(yT_ready, K2 * (done_pair + 1))
                if not (isinstance(done_pair, int) and done_pair == 0):
                    act.wait_ge(out_done, 16 * B * done_pair)
                nc.scalar.copy(o_sb[:], zbank(1, 0, 0)[:, 0:D]).then_inc(o_ready, 1)

            def states(pair, first, last):
                for s in range(PAIR):
                    if s % TS == 0 and not first:
                        act.wait_ge(y_ready, 2 * pair + s // TS - 1)
                    for m in range(K2):
                        act.wait_ge(z_ready, 2 * PAIR * pair + 2 * s + m + 1)
                        zt = zbank(s // TS, s % 2, m)[:, B * (s % TS // 2):B * (s % TS // 2 + 1)]
                        nc.scalar.activation(h_ring[:, m, s, :], zt, ACT.Tanh).then_inc(h_ready, 1)
                    if not (last and s >= TS):
                        if s % TS == 0:
                            x_part1((PAIR * pair + TS * (s // TS + 1)) * B)
                        if s % TS == 1:
                            x_part2(2 * pair + s // TS + 1)
                    if s == ROWS and not first:
                        move_rows(pair - 1)
                if last:
                    move_rows(pair)

            over_pairs(act, states)

        @block.vector
        def _(dve):
            steps = [0]

            def then_wait(ins):
                steps[0] += 1
                ins.then_inc(dve_step, 1)
                dve.wait_ge(dve_step, steps[0])

            dve.wait_ge(ld_cond, 80)
            then_wait(nc.vector.bn_stats(stats[:], cond_sb[:]))
            nc.vector.bn_aggr(mv[:], stats[:]).then_inc(var_ready, 1)
            dve.wait_ge(std_ready, 1)
            then_wait(nc.vector.reciprocal(rstd[:], std[:]))
            then_wait(nc.vector.tensor_scalar(cn[:], cond_sb[:], mv[:, 0:1], rstd[:], ALU.subtract, ALU.mult))
            then_wait(nc.vector.tensor_tensor(cn[:], cn[:], gamma_sb[:], ALU.mult))
            nc.vector.tensor_tensor(cn[:], cn[:], beta_sb[:], ALU.add).then_inc(cn_ready, 1)
            dve.wait_ge(const_ready, 4)
            nc.vector.tensor_reduce(rmask[:], sel3[:].rearrange("p q r -> p r q"), AX.X, ALU.add)
            then_wait(nc.vector.tensor_reduce(bmask[:], sel3[:].rearrange("p (j b) r -> p b j r", b=B), AX.XY,
                                              ALU.add))
            dve.wait_ge(cT_psum, 1)
            nc.vector.tensor_copy(cT[:].rearrange("p k b -> p (k b)"),
                                  bank[7][:, 16:16 + K2 * B]).then_inc(cT_ready, 1)

            nc.vector.tensor_copy(quadrant[:], ident[0:NTYPE, 0:NTYPE].unsqueeze(2).broadcast_to(
                [NTYPE, NTYPE, Q])).then_inc(quadrant_ready, 1)
            dve.wait_ge(g_ready, 2)
            nc.vector.tensor_copy(gRep[:], gT[:].unsqueeze(3).broadcast_to([P, K2, B, RANK])).then_inc(grep_ready, 1)
            dve.wait_ge(upT_psum, 1)
            nc.vector.tensor_copy(upT[:].rearrange("p k n -> p (k n)"), bank[6][:]).then_inc(upT_ready, 1)

            def keep_rank(dst, src, tmp, n):
                mask = rmask[:].unsqueeze(1).broadcast_to([P, n, RANK])
                then_wait(nc.vector.tensor_tensor(tmp.rearrange("p (d r) -> p d r", r=RANK),
                                                  src.rearrange("p (d r) -> p d r", r=RANK), mask, ALU.mult))
                then_wait(nc.vector.tensor_reduce(dst, tmp.rearrange("p (d r) -> p d r", r=RANK), AX.X, ALU.add))

            DC = CH // RANK
            for c in range(NCH):
                dve.wait_ge(w_ready, c + 1)
                keep_rank(fac[:, DC * c:DC * (c + 1)], bank[c][:], wmul[:, c % 2], DC)
            nc.vector.tensor_copy(b2s[Q * A2:Q * (A2 + 1)], fac[Q * B2:Q * (B2 + 1)]).then_inc(b2_ready, 1)
            nc.vector.tensor_tensor(facm[:], fac[:].unsqueeze(1).broadcast_to([P, B, D]),
                                    bmask[:].unsqueeze(2).broadcast_to([P, B, D]), ALU.mult).then_inc(facm_ready, 1)
            dve.wait_ge(ld_base, 16)
            def add_down(b):
                dve.wait_ge(wd_psum, b + 1)
                nc.vector.tensor_tensor(wd[:, b].rearrange("p k n -> p (k n)"), bank[4 + b][:],
                                        down_sb[:].rearrange("p k n -> p (k n)"), ALU.add).then_inc(wd_ready, 1)

            def add_up(b):
                dve.wait_ge(wu_psum, b + 1)
                nc.vector.tensor_tensor(wu[:, b].rearrange("p k n -> p (k n)"), bank[b][:],
                                        upT[:].rearrange("p k n -> p (k n)"), ALU.add).then_inc(wu_ready, 1)
            for b in range(B):
                add_down(b)
            dve.wait_ge(upT_ready, 1)
            add_up(0)
            add_up(1)
            for b in range(B):
                if b == 1:
                    add_up(2)
                    add_up(3)
                for n in range(K2):
                    dve.wait_ge(up_psum, K2 * b + n + 1)
                    nc.vector.scalar_tensor_tensor(
                        out=x2T[:, n].rearrange("p (t b) -> p b t", b=B)[:, b], in0=xT[:, n, b, :], scalar=2.0,
                        in1=bank[2 * (b % 2) + n][:], op0=ALU.mult, op1=ALU.add).then_inc(x2_ready, 1)

            def x_res1(tile_no, col0):
                dve.wait_ge(xp1_ready, tile_no + 1)
                nc.vector.tensor_tensor(x_res[:], x2T[:, :, bass.ds(col0, TC)], xp[0][:],
                                        ALU.subtract).then_inc(xr_ready, 1)

            def x_part3(tile_no):
                dve.wait_ge(xp2_ready, tile_no + 1)
                nc.vector.tensor_tensor(xp[2][:], x_res[:], xp[1][:], ALU.subtract).then_inc(xp3_ready, 1)

            x_res1(0, 0)
            x_part3(0)

            def output_sum(p, col0, in_pair):
                if p == 0 and not (isinstance(in_pair, int) and in_pair == 0):
                    dve.wait_ge(yT_ready, K2 * in_pair)
                for k in range(K2):
                    last = nc.vector.tensor_tensor(
                        y_sb[:, k, :, TS * p:TS * (p + 1)],
                        x2T[:, k, bass.ds(col0, TC)].rearrange("p (t b) -> p b t", b=B),
                        h_ring[:, k, TS * p:TS * (p + 1), :].rearrange("p t b -> p b t"), ALU.add)
                last.then_inc(y_ready, 1)

            def residues(pair, first, last):
                for s in range(PAIR):
                    q = s % 2
                    before = slot_before(s)
                    for k in range(K2):
                        dve.wait_ge(h_ready, 2 * PAIR * pair + 2 * s + k + 1)
                        nc.vector.tensor_tensor(r_ring[:, k, q, :], h_ring[:, k, before, :], h_hi[:, k, before, :],
                                                ALU.subtract).then_inc(r_ready, 1)
                    for k in range(K2):
                        dve.wait_ge(r_ready, 2 * PAIR * pair + 2 * s + k + 1)
                        nc.vector.tensor_tensor(l_ring[:, k, q, :], r_ring[:, k, q, :], r_hi[:, k, q, :],
                                                ALU.subtract).then_inc(l_ready, 1)
                    if not (last and s >= TS):
                        if s % TS == 1:
                            x_res1(2 * pair + s // TS + 1, (PAIR * pair + TS * (s // TS + 1)) * B)
                        if s % TS == 2:
                            x_part3(2 * pair + s // TS + 1)
                    if s == SUMS and not first:
                        output_sum(1, (PAIR * pair - TS) * B, pair - 1)
                    if s == TS + SUMS:
                        output_sum(0, PAIR * pair * B, pair)
                if last:
                    dve.wait_ge(h_ready, 2 * PAIR * (pair + 1) + 2)
                    output_sum(1, (PAIR * pair + TS) * B, pair)

            over_pairs(dve, residues)

        @block.tensor
        def _(pe):
            pe.wait_ge(const_ready, 4)
            pe.wait_ge(ld_cond, 80)
            for k in range(K2):
                last = nc.tensor.transpose(bank[7][:, B * k:B * (k + 1)], cond_sb[:, P * k:P * (k + 1)],
                                           ident[0:B, 0:B])
            last.then_inc(condT_ready, 1)

            def transposes(g):
                if g >= 3:
                    pe.wait_ge(tr_moved, g - 2)
                for i in range(NTT):
                    last = nc.tensor.transpose(tr_bank(g)[:, P * i:P * (i + 1)],
                                               x_sb[:, g // K2, i, P * (g % K2):P * (g % K2 + 1)], ident[:])
                last.then_inc(tr_ready, 1)

            pe.wait_ge(cn_ready, 1)
            pe.wait_ge(h_ready, 2)
            for k in range(K2):
                last = nc.tensor.transpose(bank[7][:, 16 + B * k:16 + B * (k + 1)], cn[:, P * k:P * (k + 1)],
                                           ident[0:B, 0:B])
            last.then_inc(cT_psum, 1)
            pe.wait_ge(cT_ready, 1)
            for m in range(K2):
                for k in range(K2):
                    last = nc.tensor.matmul(bank[7][:, 32 + B * m:32 + B * (m + 1)], w1_sb[:, k, P * m:P * (m + 1)],
                                            cT[:, k, :], start=(k == 0), stop=(k == K2 - 1))
            last.then_inc(hpre_ready, 1)
            pe.wait_ge(ld_up, 16)
            for i in range(K2 * K2):
                last = nc.tensor.transpose(bank[6][:, P * i:P * (i + 1)],
                                           up_sb[:, i % K2, P * (i // K2):P * (i // K2 + 1)], ident[:])
            last.then_inc(upT_psum, 1)
            pe.wait_ge(upT_ready, 1)
            for g in range(B * K2 // 2):
                if g % K2 == 0:
                    pe.wait_ge(ld_x[g // K2], 16)
                transposes(g)
            pe.wait_ge(ld_bias2, 16)
            pe.wait_ge(quadrant_ready, 1)
            for c in range(NCH):
                nc.tensor.matmul(bank[c][:], quadrant[:].rearrange("j i q -> j (i q)"),
                                 bias2_sb[:, CH * c:CH * (c + 1)], start=True, stop=False, skip_group_check=True)
            pe.wait_ge(grep_ready, 1)
            for c in range(NCH):
                for k in range(K2):
                    pe.wait_ge(ld_w2[c][k], 16)
                    for j in range(NTYPE):
                        last = nc.tensor.matmul(bank[c][Q * j:Q * (j + 1), :],
                                                gRep[:, k].rearrange("p b r -> p (b r)"),
                                                w2_sb[:, k, j, CH * c:CH * (c + 1)], start=False,
                                                stop=(k == K2 - 1), skip_group_check=True)
                last.then_inc(w_ready, 1)
            for g in range(B * K2 // 2, B * K2):
                if g % K2 == 0:
                    pe.wait_ge(ld_x[g // K2], 16)
                transposes(g)
            pe.wait_ge(b2_ready, 1)
            pe.wait_ge(facm_ready, 1)
            pe.wait_ge(tr_moved, B * K2)

            def low_down(b):
                for k in range(K2):
                    last = nc.tensor.matmul(bank[4 + b][:, D * k:D * (k + 1)],
                                            facm[Q * A2:Q * (A2 + 1), b, P * k:P * (k + 1)],
                                            b2s[Q * A2:Q * (A2 + 1), :], start=True, stop=True)
                last.then_inc(wd_psum, 1)

            def low_up(b):
                for k in range(K2):
                    last = nc.tensor.matmul(bank[b][:, D * k:D * (k + 1)], b1m[:, b, P * k:P * (k + 1)],
                                            fac[Q * A1:Q * (A1 + 1), :], start=True, stop=True)
                last.then_inc(wu_psum, 1)

            def down(b):
                pe.wait_ge(wd_ready, 2 if b == 0 else B)
                if b >= 2:
                    pe.wait_ge(mid_ready, K2 * (b - 1))
                for m in range(K2):
                    for k in range(K2):
                        last = nc.tensor.matmul(bank[4 + 2 * (b % 2) + m][:], wd[:, b, k, P * m:P * (m + 1)],
                                                xT[:, k, b, :], start=(k == 0), stop=(k == K2 - 1))
                    last.then_inc(mid_psum, 1)

            def up(b):
                pe.wait_ge(mid_ready, K2 * (b + 1))
                pe.wait_ge(wu_ready, 2 if b == 0 else B)
                if b >= 2:
                    pe.wait_ge(x2_ready, K2 * (b - 1))
                for n in range(K2):
                    for k in range(K2):
                        last = nc.tensor.matmul(bank[2 * (b % 2) + n][:], wu[:, b, k, P * n:P * (n + 1)],
                                                midT[:, b % 2, k, :], start=(k == 0), stop=(k == K2 - 1))
                    last.then_inc(up_psum, 1)

            low_down(0)
            low_down(1)
            down(0)
            low_down(2)
            low_down(3)
            pe.wait_ge(b1_ready, 1)
            low_up(0)
            low_up(1)
            down(1)
            up(0)
            low_up(2)
            low_up(3)
            for b in range(2, B):
                down(b)
                up(b - 1)
            up(B - 1)

            PAIRS6 = [(0, 0), (1, 0), (2, 0), (0, 1), (1, 1), (0, 2)]

            def input_products(p, q, m, halves, pairs=PAIRS6):
                zb = zbank(p, q, m)[:, 0:TC // 2]
                if halves[0] == 0 and pairs[0] == (0, 0):
                    nc.tensor.matmul(zb, b3h[:, P * m:P * (m + 1)], ones[:], start=True, stop=False,
                                     skip_group_check=True)
                for k in halves:
                    for w, v in pairs:
                        rhs = xp[v][:, k].rearrange("p (t q b) -> p t q b", q=2, b=B)[:, :, q, :]
                        nc.tensor.matmul(zb, wxp[w][:, k, P * m:P * (m + 1)], rhs, start=False, stop=False,
                                         skip_group_check=True)

            def output_transpose(done_pair, n):
                if n == 0:
                    pe.wait_ge(y_ready, 2 * done_pair + 2)
                    if not (isinstance(done_pair, int) and done_pair == 0):
                        pe.wait_ge(o_ready, done_pair)
                nc.tensor.transpose(zbank(1, 0, 0)[:, P * n:P * (n + 1)],
                                    y_sb[:, n].rearrange("p b t -> p (b t)"), ident[:]).then_inc(yT_ready, 1)

            def recurrence(pair, first, last):
                for s in range(PAIR):
                    p, q, before = s // TS, s % 2, slot_before(s)
                    cols = slice(B * (s % TS // 2), B * (s % TS // 2 + 1))
                    done = 2 * PAIR * pair + 2 * s

                    def product(part, k, m, rhs, stop=False):
                        return nc.tensor.matmul(zbank(p, q, m)[:, cols], whp[part][:, k, P * m:P * (m + 1)], rhs,
                                                start=False, stop=stop, skip_group_check=True)

                    for k in range(K2):
                        pe.wait_ge(h_ready, done + k + 1)
                        for m in range(K2):
                            for part in range(NPART):
                                product(part, k, m, h_hi[:, k, before, :])
                    pe.wait_ge(r_ready, done + 1)
                    for m in range(K2):
                        for part in range(2):
                            product(part, 0, m, r_hi[:, 0, q, :])
                    pe.wait_ge(r_ready, done + 2)
                    for part in range(2):
                        product(part, 1, 0, r_hi[:, 1, q, :])
                    pe.wait_ge(l_ready, done + 1)
                    product(0, 0, 0, l_ring[:, 0, q, :])
                    pe.wait_ge(l_ready, done + 2)
                    product(0, 1, 0, l_ring[:, 1, q, :], stop=True).then_inc(z_ready, 1)
                    for part in range(2):
                        product(part, 1, 1, r_hi[:, 1, q, :])
                    product(0, 0, 1, l_ring[:, 0, q, :])
                    product(0, 1, 1, l_ring[:, 1, q, :], stop=True).then_inc(z_ready, 1)

                    if TURN <= s < TURN + K2 and not first:
                        output_transpose(pair - 1, s - TURN)
                    i = s % TS - PREFETCH
                    if i >= 0 and not (last and p == 1):
                        if i == 0:
                            pe.wait_ge(xp2_ready, 2 * pair + p + 2)
                            pe.wait_ge(xp3_ready, 2 * pair + p + 2)
                            if p == 0 and not first:
                                pe.wait_ge(o_ready, pair)
                        input_products(1 - p, i // 4, i // 2 % 2, [i % 2])
                if last:
                    for n in range(K2):
                        output_transpose(pair, n)

            pe.wait_ge(wxp_ready, 1)
            pe.wait_ge(bp_ready, 1)
            for arrived, pairs in ((xp1_ready, PAIRS6[0:3]), (xp2_ready, PAIRS6[3:5]), (xp3_ready, PAIRS6[5:6])):
                pe.wait_ge(arrived, 1)
                for q in range(2):
                    for m in range(K2):
                        input_products(0, q, m, range(K2), pairs)
            pe.wait_ge(whp_ready, 1)
            over_pairs(pe, recurrence)


_INS = ["x", "cond_1024", "L0_cond_base_up", "L0_cond_base_down", "L0_cond_ln_gamma", "L0_cond_ln_beta",
        "L0_cond_W1", "L0_cond_bias1", "L0_cond_W2", "L0_cond_bias2", "L1_cond_Wx", "L1_cond_Wh", "L1_cond_b"]


def kernel(**inputs):
    import numpy as _np
    import concourse.bacc as _bacc
    from concourse import mybir as _mybir
    from concourse.bass_utils import run_bass_kernel_spmd as _run

    nc = _bacc.Bacc("TRN2", target_bir_lowering=False, num_devices=1)
    arrays, args = {}, []
    for name in _INS:
        a = _np.ascontiguousarray(inputs[name])
        arrays[f"in_{name}"] = a
        args.append(nc.dram_tensor(f"in_{name}", a.shape, _mybir.dt.from_np(a.dtype), kind="ExternalInput").ap())
    shape = inputs["x"].shape
    args.append(nc.dram_tensor("out_0", shape, _mybir.dt.float32, kind="ExternalOutput").ap())
    adaptive_lowrank_then_recurrence(nc, *args)
    r = _run(nc, [arrays], core_ids=[0])
    return r.results[0]["out_0"]
```
